# Optimizing a Trainium2 kernel written in Bass

```python
import numpy as np
import jax
import jax.numpy as jnp

def _softmax(x, axis=-1):
    return jax.nn.softmax(x, axis=axis)

def _gelu(x):
    return jax.nn.gelu(x, approximate=True)

def _silu(x):
    return jax.nn.silu(x)

def _sigmoid(x):
    return jax.nn.sigmoid(x)

def _layernorm(x, axis=-1, eps=1e-05):
    m = jnp.mean(x, axis=axis, keepdims=True)
    v = jnp.var(x, axis=axis, keepdims=True)
    return (x - m) / jnp.sqrt(v + eps)

def _scatter_add(tgt, idx, src, axis=0):
    return tgt.at[idx].add(src)

def _segment_sum(src, seg, n):
    return jax.ops.segment_sum(src, seg, n)
kernel_name = 'mk_flamingo_gated_d1_seqx_r4_c5076e'

def setup_inputs(seed: int=0):
    np.random.seed(seed)
    _w = jnp.asarray

    def _rec_inputs():
        import jax
        import jax.numpy as jnp
        _rk = jax.random.key(seed)
        x = -0.0002928 + 1 * jax.random.normal(jax.random.fold_in(_rk, 1), (64, 128, 256), jnp.float32)
        _lenS = 128 - jax.random.randint(jax.random.fold_in(_rk, 7), (64,), 0, max(1, 128 // 4) + 1, jnp.int32)
        _lenS2 = 128 - jax.random.randint(jax.random.fold_in(_rk, 8), (64,), 0, max(1, 128 // 4) + 1, jnp.int32)
        _ctx_1024P = jax.random.normal(jax.random.fold_in(_rk, 11), (64, 16, 256), jnp.float32)
        _ctx_1024c = jax.random.dirichlet(jax.random.fold_in(_rk, 511), 0.3 * jnp.ones((16,), jnp.float32), (64, 128))
        _ctx_1024t = jnp.einsum('bsk,bkd->bsd', _ctx_1024c, _ctx_1024P)
        _ctx_1024t = _ctx_1024t * jax.lax.rsqrt(jnp.mean(jnp.square(_ctx_1024t)) + 1e-12) * 0.953939
        ctx_1024 = 4.13588e-05 + 0.999923 * (_ctx_1024t + 0.3 * jax.random.normal(jax.random.fold_in(_rk, 611), (64, 128, 256), jnp.float32))
        _validS = jnp.arange(128)[None, :] < _lenS[:, None]
        _validS2 = jnp.arange(128)[None, :] < _lenS2[:, None]
        _causal = jnp.tril(jnp.ones((128, 128), dtype=bool))
        mask_Bx1x1xS2_ff0 = jnp.where(jnp.ones((64, 1, 1, 128), dtype=bool), 0.0, -1000000000.0).astype(jnp.float32)
        _g = jax.random.normal(jax.random.fold_in(_rk, 9001), (2, 1), jnp.float32)
        _g = jnp.sign(_g) * jnp.maximum(jnp.abs(_g), 1.0) + (_g == 0) * 1.0
        g_xattn = _g[0]
        g_ffn = _g[1]
        return (x, ctx_1024, mask_Bx1x1xS2_ff0, g_xattn, g_ffn)
    x, ctx_1024, mask_Bx1x1xS2_ff0, g_xattn, g_ffn = _rec_inputs()

    def _L0_xattn_setup():
        import jax, jax.numpy as jnp
        import numpy as np
        N_HEAD = 16

        def _split_heads(t):
            B, S, D = t.shape
            return t.reshape(B, S, N_HEAD, D // N_HEAD).transpose(0, 2, 1, 3)
        key = jax.random.key(seed)
        ks = jax.random.split(key, 8)
        B, Sq, Sk, D = (4, 256, 512, 256)
        s = 0.02
        return {'x': jax.random.normal(ks[0], (B, Sq, D), jnp.float32), 'ctx': jax.random.normal(ks[1], (B, Sk, D), jnp.float32), 'attention_mask': jnp.zeros((B, 1, 1, Sk), jnp.float32), 'Wq': jax.random.normal(ks[2], (D, D), jnp.float32) * s, 'bq': jnp.zeros((D,), jnp.float32), 'Wkv': jax.random.normal(ks[3], (D, 2 * D), jnp.float32) * s, 'bkv': jnp.zeros((2 * D,), jnp.float32), 'Wp': jax.random.normal(ks[4], (D, D), jnp.float32) * s, 'bp': jnp.zeros((D,), jnp.float32)}
    _L0_xattn_all = _L0_xattn_setup()
    _L0_xattn_in = {k: v for k, v in _L0_xattn_all.items() if k in ('Wq', 'bq', 'Wkv', 'bkv', 'Wp', 'bp')}
    del _L0_xattn_all

    def _L0_ffn_setup():
        import jax, jax.numpy as jnp
        import numpy as np
        B, S, D, H, E, K = (4, 512, 256, 512, 8, 2)
        TEMP = 5.0
        EPS = 1e-09
        key = jax.random.key(seed)
        k_x, k_wg, k_w1, k_w2 = jax.random.split(key, 4)
        scale = 0.02
        return {'x': jax.random.normal(k_x, (B, S, D), dtype=jnp.float32), 'Wg': jax.random.normal(k_wg, (D, E), dtype=jnp.float32) * scale, 'bg': jnp.zeros((E,), dtype=jnp.float32), 'W1': jax.random.normal(k_w1, (E, D, H), dtype=jnp.float32) * scale, 'b1': jnp.zeros((E, H), dtype=jnp.float32), 'W2': jax.random.normal(k_w2, (E, H, D), dtype=jnp.float32) * scale, 'b2': jnp.zeros((E, D), dtype=jnp.float32)}
    _L0_ffn_all = _L0_ffn_setup()
    _L0_ffn_in = {k: v for k, v in _L0_ffn_all.items() if k in ('Wg', 'bg', 'W1', 'b1', 'W2', 'b2')}
    del _L0_ffn_all
    return {'x': x, 'ctx_1024': ctx_1024, 'mask_Bx1x1xS2_ff0': mask_Bx1x1xS2_ff0, 'g_xattn': g_xattn, 'g_ffn': g_ffn, 'L0_xattn_Wq': _L0_xattn_in['Wq'], 'L0_xattn_bq': _L0_xattn_in['bq'], 'L0_xattn_Wkv': _L0_xattn_in['Wkv'], 'L0_xattn_bkv': _L0_xattn_in['bkv'], 'L0_xattn_Wp': _L0_xattn_in['Wp'], 'L0_xattn_bp': _L0_xattn_in['bp'], 'L0_ffn_Wg': _L0_ffn_in['Wg'], 'L0_ffn_bg': _L0_ffn_in['bg'], 'L0_ffn_W1': _L0_ffn_in['W1'], 'L0_ffn_b1': _L0_ffn_in['b1'], 'L0_ffn_W2': _L0_ffn_in['W2'], 'L0_ffn_b2': _L0_ffn_in['b2']}

def reference(x, ctx_1024, mask_Bx1x1xS2_ff0, g_xattn, g_ffn, L0_xattn_Wq, L0_xattn_bq, L0_xattn_Wkv, L0_xattn_bkv, L0_xattn_Wp, L0_xattn_bp, L0_ffn_Wg, L0_ffn_bg, L0_ffn_W1, L0_ffn_b1, L0_ffn_W2, L0_ffn_b2):
    import jax
    import jax.numpy as jnp

    def _L0_xattn_ref(x, ctx, attention_mask, Wq, bq, Wkv, bkv, Wp, bp):
        import jax, jax.numpy as jnp
        import numpy as np
        N_HEAD = 16

        def _split_heads(t):
            B, S, D = t.shape
            return t.reshape(B, S, N_HEAD, D // N_HEAD).transpose(0, 2, 1, 3)
        B, Sq, D = x.shape
        dh = D // N_HEAD
        q = _split_heads(x @ Wq + bq)
        kv = ctx @ Wkv + bkv
        k = _split_heads(kv[..., :D])
        v = _split_heads(kv[..., D:])
        w = jnp.einsum('bhqd,bhkd->bhqk', q, k) / jnp.sqrt(jnp.float32(dh))
        w = w + attention_mask
        w = jax.nn.softmax(w, axis=-1)
        a = jnp.einsum('bhqk,bhkd->bhqd', w, v)
        a = a.transpose(0, 2, 1, 3).reshape(B, Sq, D)
        return a @ Wp + bp

    def _L0_ffn_ref(x, Wg, bg, W1, b1, W2, b2):
        import jax, jax.numpy as jnp
        import numpy as np
        B, S, D, H, E, K = (4, 512, 256, 512, 8, 2)
        TEMP = 5.0
        EPS = 1e-09
        logits = jnp.einsum('bsd,de->bse', x, Wg) + bg
        probs = jax.nn.softmax(logits / TEMP, axis=-1)
        vals, idx = jax.lax.top_k(probs, K)
        onehot = jax.nn.one_hot(idx, E, dtype=x.dtype)
        mask = jnp.einsum('bske,bsk->bse', onehot, vals)
        gates = mask / (jnp.sum(mask, axis=-1, keepdims=True) + EPS)
        h = jax.nn.gelu(jnp.einsum('bsd,edh->besh', x, W1) + b1[None, :, None, :], approximate=False)
        out = jnp.einsum('besh,ehd->besd', h, W2) + b2[None, :, None, :]
        y = jnp.einsum('bse,besd->bsd', gates, out)
        return y
    x = x + jnp.tanh(g_xattn[0]) * _L0_xattn_ref(_layernorm(x, axis=-1), ctx_1024, mask_Bx1x1xS2_ff0, L0_xattn_Wq, L0_xattn_bq, L0_xattn_Wkv, L0_xattn_bkv, L0_xattn_Wp, L0_xattn_bp)
    x = x + jnp.tanh(g_ffn[0]) * _L0_ffn_ref(_layernorm(x, axis=-1), L0_ffn_Wg, L0_ffn_bg, L0_ffn_W1, L0_ffn_b1, L0_ffn_W2, L0_ffn_b2)
    return x

_drawn_inputs = setup_inputs


def setup_inputs(seed=0):
    import zlib

    import numpy as np

    out = dict(_drawn_inputs(seed))
    spreads = {'L0_xattn_bq': (0.0, 2.0),
     'L0_xattn_bkv': (0.0, 0.29),
     'L0_xattn_bp': (0.0, 0.1),
     'L0_ffn_bg': (0.0, 0.1),
     'L0_ffn_b1': (0.0, 0.481),
     'L0_ffn_b2': (0.0, 0.1)}
    factors = {'L0_xattn_Wq': 24.579}
    for name, (base, spread) in spreads.items():
        noise = np.random.default_rng([zlib.crc32(name.encode()), seed]).standard_normal(out[name].shape)
        drawn = base * np.exp(spread * noise) if base else spread * noise
        out[name] = jnp.asarray(drawn.astype(out[name].dtype))
    for name, factor in factors.items():
        out[name] = (out[name] * factor).astype(out[name].dtype)
    return out
```

```python
from contextlib import ExitStack

import concourse.bass as bass
from concourse import mybir

F32 = mybir.dt.float32
U32 = mybir.dt.uint32
ALU = mybir.AluOpType
ACT = mybir.ActivationFunctionType
AX_X = mybir.AxisListType.X

P = 128
G = 4
NH = 16
DH = 16
HC = P // DH
KC = 2
LN_EPS = 1e-5
TEMP = 5.0
GATE_EPS = 1e-9
UNITS = G * KC


class Signal:

    def __init__(self, handle, per, credit, step):
        self.handle, self.per, self.credit, self.step = handle, per, credit, step

    def at(self, i, k):
        return i * (self.per * self.step) + (k + self.credit) * self.step


def gated_xattn_moe(nc, x, ctx_in, mask, g_xattn, g_ffn, Wq, bq, Wkv, bkv, Wp, bp, Wg, bg, W1, b1, W2, b2, out):
    NB, S, D = x.shape
    E, _, H = W1.shape
    NG = NB // G
    HK = H // P
    assert S == P and D == KC * P and ctx_in.shape[1] == P and NH * DH == D

    with ExitStack() as stack:
        def sb(name, shape, dt=F32):
            return stack.enter_context(nc.sbuf_tensor(name, shape, dt))

        def ps(name, shape):
            return stack.enter_context(nc.psum_tensor(name, shape, F32))

        def signal(name, per=1, credit=0, step=1):
            return Signal(stack.enter_context(nc.semaphore(name)), per, credit, step)

        def give_credit(eng, *signals):
            for sig in signals:
                eng.sem_inc(sig.handle, sig.credit * sig.step)

        wq = sb("wq", [P, KC, D])
        wkv = sb("wkv", [P, KC, 2 * D])
        wp = sb("wp", [P, KC, D])
        wg = sb("wg", [P, KC, E])
        w1 = sb("w1", [P, E, KC, H])
        w2 = sb("w2", [P, E, HK, D])
        b1c = sb("b1c", [P, E, HK])
        bqk = sb("bqk", [P, 2, KC])
        bv_row = sb("bv_row", [P, D])
        bp_row = sb("bp_row", [P, D])
        bg_row = sb("bg_row", [P, E])
        b2_e = sb("b2_e", [E, D])
        gate_in = sb("gate_in", [P, 2])
        gate_tanh = sb("gate_tanh", [P, 2])
        tbp_row = sb("tbp_row", [P, D])
        ident = sb("ident", [P, P])
        head_mask = sb("head_mask", [P, HC])
        bq4 = sb("bq4", [P, KC])
        half = sb("half", [P, G])
        expert_no = sb("expert_no", [P, E])

        xg = sb("xg", [P, G, D])
        cg = sb("cg", [P, G, D])
        mg = sb("mg", [P, G, P])
        stat = sb("stat", [P, G, 6])
        mv = sb("mv", [P, G, 2])
        var_eps = sb("var_eps", [P, G])
        rstd = sb("rstd", [P, G])
        xn = sb("xn", [P, G, D])
        xb = sb("xb", [P, G, D])
        xT = sb("xT", [P, KC, G * P])
        cT = sb("cT", [P, KC, G * P])
        qT = sb("qT", [P, KC, G * P])
        kT = sb("kT", [P, KC, G * P])
        v = sb("v", [P, G, D])
        vbd = sb("vbd", [P, 2, NH, P])
        kbd = sb("kbd", [P, 2, HC, P])
        s = sb("s", [P, 3, HC, P])
        nmax = sb("nmax", [P, 2, HC])
        z = sb("z", [P, 2, HC])
        rz = sb("rz", [P, 2, HC, DH])
        pT = sb("pT", [P, 2, 2, 4 * P])
        rzT = sb("rzT", [P, KC, P])
        aT = sb("aT", [P, KC, P])
        x1 = sb("x1", [P, G, D])
        stat2 = sb("stat2", [P, G, 6])
        mv2 = sb("mv2", [P, G, 2])
        var_eps2 = sb("var_eps2", [P, G])
        rstd2 = sb("rstd2", [P, G])
        xn2 = sb("xn2", [P, G, D])
        x2T = sb("x2T", [P, KC, G * P])
        logit = sb("logit", [P, G, E])
        nlmax = sb("nlmax", [P, G])
        prob = sb("prob", [P, G, E])
        top = sb("top", [P, G, 8])
        topi = sb("topi", [P, G, 8], U32)
        topf = sb("topf", [P, G, 2])
        one1 = sb("one1", [P, G, E])
        one2 = sb("one2", [P, G, E])
        gsum = sb("gsum", [P, G])
        gate = sb("gate", [P, G, E])
        gateT = sb("gateT", [E, G, P])
        hT = sb("hT", [P, 2, HK, G * P])

        psS = ps("psS", [P, 2, HC, P])
        psP = ps("psP", [P, 2, 4 * P])
        psA = ps("psA", [P, 4, P])
        psW = ps("psW", [P, 512])
        bank = [psS[:, j // 2, 4 * (j % 2):4 * (j % 2) + 4, :].rearrange("p h k -> p (h k)") for j in range(4)]

        w_ld = signal("w_ld")
        mask_set = signal("mask_set")
        const = signal("const")
        dconst = signal("dconst")
        tanh_rdy = signal("tanh_rdy")
        x_ld = signal("x_ld", step=16)
        c_ld = signal("c_ld", step=16)
        m_ld = signal("m_ld", step=16)
        mv_rdy = signal("mv_rdy")
        rstd_rdy = signal("rstd_rdy", 1)
        xn_rdy = signal("xn_rdy", 1, credit=1)
        xb_rdy = signal("xb_rdy", 1, credit=1)
        st1 = signal("st1", 10, credit=1)
        ev1 = signal("ev1", 8)
        v_rdy = signal("v_rdy", 2)
        kbd_rdy = signal("kbd_rdy", UNITS)
        vbd_rdy = signal("vbd_rdy", UNITS, credit=1)
        s_rdy = signal("s_rdy", UNITS, credit=2)
        sm_rdy = signal("sm_rdy", UNITS, credit=1)
        mx_rdy = signal("mx_rdy", UNITS)
        p_rdy = signal("p_rdy", UNITS, credit=2)
        rz_rdy = signal("rz_rdy", UNITS, credit=2)
        pt_rdy = signal("pt_rdy", 2 * UNITS, credit=5)
        ptd = signal("ptd", UNITS, credit=1)
        pta = signal("pta", UNITS, credit=1)
        pv_rdy = signal("pv_rdy", UNITS, credit=4)
        r_rdy = signal("r_rdy", G, credit=1)
        r_ev = signal("r_ev", G)
        a_rdy = signal("a_rdy", G, credit=1)
        proj_rdy = signal("proj_rdy", G, credit=1)
        x1_rdy = signal("x1_rdy", G, credit=1)
        mv2_rdy = signal("mv2_rdy")
        rstd2_rdy = signal("rstd2_rdy")
        xn2_rdy = signal("xn2_rdy")
        t2_rdy = signal("t2_rdy", KC)
        t2_ev = signal("t2_ev", KC)
        lg_rdy = signal("lg_rdy")
        lm_rdy = signal("lm_rdy")
        ex_rdy = signal("ex_rdy")
        gate_rdy = signal("gate_rdy")
        gt_rdy = signal("gt_rdy")
        gt_ev = signal("gt_ev")
        yb_rdy = signal("yb_rdy", G // 2)
        yb_ev = signal("yb_ev", G // 2, credit=1)
        h_rdy = signal("h_rdy", E * HK)
        h_act = signal("h_act", E * HK, credit=1)
        y_rdy = signal("y_rdy", E * G)
        y_add = signal("y_add", E * G, credit=1)
        stored = signal("stored", step=16)
        act_step = signal("act_step")
        passed = signal("passed")
        pool_step = signal("pool_step", 2)

        xr = x.rearrange("(n g) s d -> n s g d", g=G)
        cr = ctx_in.rearrange("(n g) s d -> n s g d", g=G)
        outr = out.rearrange("(n g) s d -> n s g d", g=G)
        mr = mask.rearrange("(n g) a b k -> n (a b) (g k)", g=G)

        block = stack.enter_context(nc.Block())

        def strided(ap, n, step, m):
            w = ap.shape[-1]
            assert (n - 1) * step + m <= w
            return bass.AP(ap.tensor, ap.offset, [ap.ap[0], [step, n], [1, m]])

        N_W = 17

        def pass_gate(eng):
            eng.sem_inc(passed.handle, 1)

        @block.sync
        def _(sp):
            loads = [
                (wq[:], Wq.rearrange("(c p) n -> p c n", p=P)),
                (wkv[:], Wkv.rearrange("(c p) n -> p c n", p=P)),
                (wp[:], Wp.rearrange("(c p) n -> p c n", p=P)),
                (wg[:], Wg.rearrange("(c p) n -> p c n", p=P)),
                (bqk[:, 0, :], bq.rearrange("(c p) -> p c", p=P)),
                (bqk[:, 1, :], bkv[0:D].rearrange("(c p) -> p c", p=P)),
                (bv_row[:], bkv[D:2 * D].rearrange("(a n) -> a n", a=1).to_broadcast([P, D])),
                (bp_row[:], bp.rearrange("(a n) -> a n", a=1).to_broadcast([P, D])),
                (bg_row[:], bg.rearrange("(a n) -> a n", a=1).to_broadcast([P, E])),
                (b2_e[:], b2),
                (gate_in[:, 0:1], g_xattn.rearrange("(a n) -> a n", a=1).to_broadcast([P, 1])),
                (gate_in[:, 1:2], g_ffn.rearrange("(a n) -> a n", a=1).to_broadcast([P, 1])),
                (b1c[:], b1.rearrange("e (c p) -> p e c", p=P)),
                (w1[:, 0:E // 2], W1[0:E // 2].rearrange("e (c p) n -> p e c n", p=P)),
                (w2[:, 0:E // 2], W2[0:E // 2].rearrange("e (c p) n -> p e c n", p=P)),
                (w1[:, E // 2:], W1[E // 2:].rearrange("e (c p) n -> p e c n", p=P)),
                (w2[:, E // 2:], W2[E // 2:].rearrange("e (c p) n -> p e c n", p=P)),
            ]
            assert len(loads) == N_W
            with nc.allow_non_contiguous_dma(reason="bias columns, once"):
                for dst, src in loads:
                    sp.dma_start(dst, src).then_inc(w_ld.handle, 16)
            with sp.Fori(0, NG) as i:
                sp.wait_ge(xb_rdy.handle, xb_rdy.at(i, 0))
                sp.wait_ge(xn_rdy.handle, xn_rdy.at(i, 0))
                sp.dma_start(xg[:], xr[i]).then_inc(x_ld.handle, 16)
                sp.wait_ge(st1.handle, st1.at(i, 0))
                sp.dma_start(cg[:], cr[i]).then_inc(c_ld.handle, 16)
                sp.wait_ge(sm_rdy.handle, sm_rdy.at(i, 0))
                sp.dma_start(mg[:].rearrange("p g k -> p (g k)"), mr[i].to_broadcast([P, G * P])).then_inc(m_ld.handle, 16)

        @block.gpsimd
        def _(pool):
            n = 0
            pool.memset(ident[:], 0.0).then_inc(const.handle, 1)
            pool.memset(head_mask[:], 1.0).then_inc(const.handle, 1)
            pool.memset(vbd[:], 0.0).then_inc(const.handle, 1)
            pool.memset(half[:], -0.5).then_inc(const.handle, 1)
            pool.iota(expert_no[:], pattern=[[1, E]], base=0, channel_multiplier=0,
                      allow_small_or_imprecise_dtypes=True).then_inc(const.handle, 1)
            pool.wait_ge(const.handle, 5)
            pool.affine_select(out=ident[:], in_=ident[:], compare_op=ALU.not_equal, fill=1.0, base=0,
                               pattern=[[-1, P]], channel_multiplier=1).then_inc(const.handle, 1)
            pool.affine_select(out=head_mask[:], in_=head_mask[:], compare_op=ALU.is_ge, fill=0.0, base=0,
                               pattern=[[-DH, HC]], channel_multiplier=1).then_inc(const.handle, 1)
            pool.wait_ge(const.handle, 7)
            pool.affine_select(out=head_mask[:], in_=head_mask[:], compare_op=ALU.is_ge, fill=0.0, base=DH - 1,
                               pattern=[[DH, HC]], channel_multiplier=-1).then_inc(const.handle, 1)
            pool.wait_ge(const.handle, 8)
            give_credit(pool, xb_rdy, vbd_rdy)
            pool.wait_ge(w_ld.handle, 16 * N_W)
            pool.wait_ge(tanh_rdy.handle, 1)
            pool.tensor_scalar(tbp_row[:], bp_row[:], gate_tanh[:, 0:1], None, ALU.mult).then_inc(const.handle, 1)
            pool.wait_ge(const.handle, 9)
            with pool.Fori(0, NG) as i:
                pool.wait_ge(mv_rdy.handle, mv_rdy.at(i, 1))
                pass_gate(pool)
                pool.tensor_scalar(var_eps[:], mv[:, :, 1], LN_EPS, None, ALU.add).then_inc(pool_step.handle, 1)
                pool.wait_ge(pool_step.handle, pool_step.at(i, 1))
                pool.tensor_tensor(rstd[:], var_eps[:], half[:], ALU.pow).then_inc(rstd_rdy.handle, 1)
                pool.wait_ge(x1_rdy.handle, x1_rdy.at(i, 0))
                pool.tensor_tensor(xb[:], xg[:], tbp_row[:].unsqueeze(1).to_broadcast([P, G, D]), ALU.add).then_inc(xb_rdy.handle, 1)
                for u in range(UNITS):
                    b, c = u // KC, u % KC
                    if u == 0:
                        pool.wait_ge(ev1.handle, ev1.at(i, 8))
                    pool.wait_ge(s_rdy.handle, s_rdy.at(i, u - 1))
                    pool.tensor_tensor(kbd[:, u % 2], kT[:, c, b * P:(b + 1) * P].unsqueeze(1).to_broadcast([P, HC, P]),
                                       head_mask[:].unsqueeze(2).to_broadcast([P, HC, P]), ALU.mult).then_inc(kbd_rdy.handle, 1)
                    if u == 0:
                        pool.wait_ge(v_rdy.handle, v_rdy.at(i, 2))
                    pool.wait_ge(pv_rdy.handle, pv_rdy.at(i, u - 3))
                    pass_gate(pool)
                    dst = vbd[:, b % 2, c * HC:(c + 1) * HC, :].rearrange("p h k -> p (h k)")
                    pool.tensor_copy(strided(dst, HC, P + DH, DH), v[:, b, c * P:(c + 1) * P].rearrange("p (h d) -> p h d", h=HC)
                                     ).then_inc(vbd_rdy.handle, 1)
                pool.wait_ge(mv2_rdy.handle, mv2_rdy.at(i, 1))
                pass_gate(pool)
                pool.tensor_scalar(var_eps2[:], mv2[:, :, 1], LN_EPS, None, ALU.add).then_inc(pool_step.handle, 1)
                pool.wait_ge(pool_step.handle, pool_step.at(i, 2))
                pool.tensor_tensor(rstd2[:], var_eps2[:], half[:], ALU.pow).then_inc(rstd2_rdy.handle, 1)
                pool.wait_ge(y_add.handle, y_add.at(i, E * G))
                pass_gate(pool)
                pool.dma_start(outr[i], x1[:]).then_inc(stored.handle, 16)
                pool.wait_ge(stored.handle, stored.at(i, 1))

        @block.scalar
        def _(act):
            act.wait_ge(w_ld.handle, 16 * N_W)
            act.activation(gate_tanh[:], gate_in[:], ACT.Tanh).then_inc(tanh_rdy.handle, 1)
            act.activation(bq4[:], bqk[:, 0, :], ACT.Copy, scale=0.25).then_inc(act_step.handle, 1)
            act.wait_ge(act_step.handle, 1)
            give_credit(act, p_rdy, h_act, pta)
            with act.Fori(0, NG) as i:
                for j in range(8):
                    act.wait_ge(st1.handle, st1.at(i, j + 1))
                    c = j % 2
                    if j < 4:
                        dst = (xT, cT)[j // 2]
                        act.activation(dst[:, c], bank[j % 4], ACT.Copy).then_inc(ev1.handle, 1)
                    elif j < 6:
                        act.activation(qT[:, c], bank[j % 4], ACT.Identity, bias=bq4[:, c:c + 1], scale=0.25).then_inc(ev1.handle, 1)
                    else:
                        act.activation(kT[:, c], bank[j % 4], ACT.Identity, bias=bqk[:, 1, c:c + 1]).then_inc(ev1.handle, 1)

                def second_half(u):
                    act.wait_ge(pt_rdy.handle, pt_rdy.at(i, 2 * u + 2))
                    act.wait_ge(pv_rdy.handle, pv_rdy.at(i, u - 1))
                    act.activation(pT[:, u % 2, 1], psP[:, 1], ACT.Copy).then_inc(pta.handle, 1)
                    if u % 2 == 1:
                        b = u // 2
                        act.wait_ge(r_rdy.handle, r_rdy.at(i, b + 1))
                        act.wait_ge(a_rdy.handle, a_rdy.at(i, b))
                        act.activation(rzT[:].rearrange("p c k -> p (c k)"), psA[:, 2:4].rearrange("p c k -> p (c k)"),
                                       ACT.Copy).then_inc(r_ev.handle, 1)

                for u in range(UNITS):
                    act.wait_ge(mx_rdy.handle, mx_rdy.at(i, u + 1))
                    act.wait_ge(rz_rdy.handle, rz_rdy.at(i, u - 1))
                    for h in range(HC):
                        ins = act.activation(s[:, u % 3, h], s[:, u % 3, h], ACT.Exp, bias=nmax[:, u % 2, h:h + 1],
                                             accum_out=z[:, u % 2, h:h + 1])
                    ins.then_inc(p_rdy.handle, 1)
                    if u > 0:
                        second_half(u - 1)
                second_half(UNITS - 1)
                for c in range(KC):
                    act.wait_ge(t2_rdy.handle, t2_rdy.at(i, c + 1))
                    act.activation(x2T[:, c], bank[c], ACT.Copy).then_inc(t2_ev.handle, 1)
                act.wait_ge(lm_rdy.handle, lm_rdy.at(i, 1))
                act.activation(prob[:], logit[:], ACT.Exp, scale=1.0 / TEMP).then_inc(ex_rdy.handle, 1)
                act.wait_ge(gt_rdy.handle, gt_rdy.at(i, 1))
                act.activation(gateT[:].rearrange("e g k -> e (g k)"), bank[2][0:E, :], ACT.Copy).then_inc(gt_ev.handle, 1)
                for e in range(E):
                    for m in range(HK):
                        n = e * HK + m
                        act.wait_ge(h_rdy.handle, h_rdy.at(i, n + 1))
                        if m == 0 and e > 1:
                            act.wait_ge(y_rdy.handle, y_rdy.at(i, (e - 1) * G))
                        act.activation(hT[:, e % 2, m], bank[n % 4], ACT.Gelu, bias=b1c[:, e, m:m + 1]).then_inc(h_act.handle, 1)

        @block.vector
        def _(dve):
            give_credit(dve, xn_rdy, sm_rdy, rz_rdy, ptd, a_rdy, x1_rdy, yb_ev, y_add)
            dve_step = signal("dve_step")
            DVE_STEPS = 23
            steps = [0]

            def link(ins, i, alone=False):
                steps[0] += 1
                ins.then_inc(dve_step.handle, 1)
                dve.wait_ge(dve_step.handle, i * DVE_STEPS + steps[0])
                if alone:
                    pass_gate(dve)

            def mark(ins):
                steps[0] += 1
                ins.then_inc(dve_step.handle, 1)

            def fence(i):
                dve.wait_ge(dve_step.handle, i * DVE_STEPS + steps[0])

            dve.wait_ge(w_ld.handle, 16 * N_W)
            dve.wait_ge(tanh_rdy.handle, 1)
            dve.wait_ge(const.handle, 9)
            with dve.Fori(0, NG) as i:
                dve.wait_ge(x_ld.handle, x_ld.at(i, 1))
                for b in range(G):
                    ins = dve.bn_stats(stat[:, b], xg[:, b])
                link(ins, i, alone=True)
                for b in range(G):
                    ins = dve.bn_aggr(mv[:, b], stat[:, b])
                ins.then_inc(mv_rdy.handle, 1)
                dve.wait_ge(mv_rdy.handle, mv_rdy.at(i, 1))
                dve.wait_ge(rstd_rdy.handle, rstd_rdy.at(i, 1))
                for b in range(G):
                    ins = dve.tensor_scalar(xn[:, b], xg[:, b], mv[:, b, 0:1], rstd[:, b:b + 1], ALU.subtract, ALU.mult)
                ins.then_inc(xn_rdy.handle, 1)
                for j in range(2):
                    dve.wait_ge(st1.handle, st1.at(i, 9 + j))
                    if j == 0:
                        dve.wait_ge(vbd_rdy.handle, vbd_rdy.at(i, 0))
                    dve.tensor_tensor(v[:, 2 * j:2 * j + 2], bank[j].rearrange("p (b n) -> p b n", b=2),
                                      bv_row[:].unsqueeze(1).to_broadcast([P, 2, D]), ALU.add).then_inc(v_rdy.handle, 1)
                dve.wait_ge(m_ld.handle, m_ld.at(i, 1))

                def row_max(u):
                    b = u // KC
                    dve.wait_ge(s_rdy.handle, s_rdy.at(i, u + 1))
                    dve.wait_ge(pt_rdy.handle, pt_rdy.at(i, 2 * u - 4))
                    dve.tensor_tensor(s[:, u % 3], psS[:, u % 2], mg[:, b].unsqueeze(1).to_broadcast([P, HC, P]),
                                      ALU.add).then_inc(sm_rdy.handle, 1)
                    dve.wait_ge(sm_rdy.handle, sm_rdy.at(i, u + 1))
                    dve.wait_ge(p_rdy.handle, p_rdy.at(i, u - 1))
                    dve.tensor_reduce(nmax[:, u % 2], s[:, u % 3], AX_X, ALU.max, negate=True).then_inc(mx_rdy.handle, 1)

                def residual(b):
                    dve.wait_ge(proj_rdy.handle, proj_rdy.at(i, b + 1))
                    if b == 0:
                        dve.wait_ge(xb_rdy.handle, xb_rdy.at(i, 1))
                    dve.scalar_tensor_tensor(x1[:, b], psW[:, 0:D], gate_tanh[:, 0:1], xb[:, b], ALU.mult, ALU.add
                                             ).then_inc(x1_rdy.handle, 1)

                def first_half(u):
                    dve.wait_ge(p_rdy.handle, p_rdy.at(i, u + 1))
                    dve.wait_ge(r_rdy.handle, r_rdy.at(i, u // 2))
                    dve.reciprocal(rz[:, u % 2], z[:, u % 2].unsqueeze(2).to_broadcast([P, HC, DH])).then_inc(rz_rdy.handle, 1)
                    dve.wait_ge(pt_rdy.handle, pt_rdy.at(i, 2 * u + 1))
                    dve.wait_ge(pv_rdy.handle, pv_rdy.at(i, u - 1))
                    dve.tensor_copy(pT[:, u % 2, 0], psP[:, 0]).then_inc(ptd.handle, 1)

                def normalize(b):
                    dve.wait_ge(pv_rdy.handle, pv_rdy.at(i, 2 * b + 2))
                    dve.wait_ge(r_ev.handle, r_ev.at(i, b + 1))
                    dve.wait_ge(proj_rdy.handle, proj_rdy.at(i, b))
                    dve.tensor_tensor(aT[:], psA[:, 0:2], rzT[:], ALU.mult).then_inc(a_rdy.handle, 1)

                row_max(0)
                for u in range(UNITS):
                    if u + 1 < UNITS:
                        row_max(u + 1)
                    first_half(u)
                    if u >= 2 and u % 2 == 0:
                        normalize(u // 2 - 1)
                    if u >= 3 and u % 2 == 1:
                        residual(u // 2 - 1)
                normalize(G - 1)
                residual(G - 1)
                dve.wait_ge(x1_rdy.handle, x1_rdy.at(i, G))
                for b in range(G):
                    ins = dve.bn_stats(stat2[:, b], x1[:, b])
                link(ins, i, alone=True)
                for b in range(G):
                    ins = dve.bn_aggr(mv2[:, b], stat2[:, b])
                ins.then_inc(mv2_rdy.handle, 1)
                dve.wait_ge(mv2_rdy.handle, mv2_rdy.at(i, 1))
                dve.wait_ge(rstd2_rdy.handle, rstd2_rdy.at(i, 1))
                for b in range(G):
                    ins = dve.tensor_scalar(xn2[:, b], x1[:, b], mv2[:, b, 0:1], rstd2[:, b:b + 1], ALU.subtract, ALU.mult)
                ins.then_inc(xn2_rdy.handle, 1)
                dve.wait_ge(lg_rdy.handle, lg_rdy.at(i, 1))
                link(dve.tensor_tensor(logit[:], psW[:, 0:G * E].rearrange("p (g e) -> p g e", g=G),
                                       bg_row[:].unsqueeze(1).to_broadcast([P, G, E]), ALU.add), i)
                link(dve.tensor_reduce(nlmax[:], logit[:], AX_X, ALU.max), i)
                dve.tensor_tensor(logit[:], logit[:], nlmax[:].unsqueeze(2).to_broadcast([P, G, E]), ALU.subtract
                                  ).then_inc(lm_rdy.handle, 1)
                dve.wait_ge(ex_rdy.handle, ex_rdy.at(i, 1))
                pass_gate(dve)
                for b in range(G):
                    link(dve.max(top[:, b], prob[:, b]), i, alone=True)
                    mark(dve.max_index(topi[:, b], top[:, b], prob[:, b]))
                fence(i)
                link(dve.tensor_copy(topf[:], topi[:, :, 0:2]), i)
                mark(dve.tensor_tensor(gsum[:], top[:, :, 0], top[:, :, 1], ALU.add))
                for k, one in enumerate((one1, one2)):
                    link(dve.tensor_tensor(one[:], expert_no[:].unsqueeze(1).to_broadcast([P, G, E]),
                                           topf[:, :, k:k + 1].to_broadcast([P, G, E]), ALU.is_equal), i)
                    mark(dve.tensor_tensor(one[:], one[:], top[:, :, k:k + 1].to_broadcast([P, G, E]), ALU.mult))
                fence(i)
                link(dve.tensor_tensor(gate[:], one1[:], one2[:], ALU.add), i)
                mark(dve.tensor_reduce(nlmax[:], prob[:], AX_X, ALU.add))
                fence(i)
                link(dve.scalar_tensor_tensor(gsum[:], nlmax[:], GATE_EPS, gsum[:], ALU.mult, ALU.add), i)
                link(dve.reciprocal(nlmax[:], gsum[:]), i)
                link(dve.tensor_scalar(nlmax[:], nlmax[:], gate_tanh[:, 1:2], None, ALU.mult), i)
                dve.tensor_tensor(gate[:], gate[:], nlmax[:].unsqueeze(2).to_broadcast([P, G, E]), ALU.mult
                                  ).then_inc(gate_rdy.handle, 1)
                for j in range(G // 2):
                    dve.wait_ge(yb_rdy.handle, yb_rdy.at(i, j + 1))
                    dve.tensor_tensor(x1[:, 2 * j:2 * j + 2], x1[:, 2 * j:2 * j + 2], psW[:].rearrange("p (b n) -> p b n", b=2), ALU.add
                                      ).then_inc(yb_ev.handle, 1)
                dve.wait_ge(yb_ev.handle, yb_ev.at(i, G // 2))
                dve.wait_ge(gate_rdy.handle, gate_rdy.at(i, 1))
                for e in range(E):
                    for b in range(G):
                        n = e * G + b
                        dve.wait_ge(y_rdy.handle, y_rdy.at(i, n + 1))
                        if e:
                            dve.wait_ge(y_add.handle, y_add.at(i, n - G + 1))
                        dve.scalar_tensor_tensor(x1[:, b], psP[:, n % 2, 0:D], gate[:, b, e:e + 1], x1[:, b], ALU.mult, ALU.add
                                                 ).then_inc(y_add.handle, 1)
            assert steps[0] == DVE_STEPS, steps[0]

        @block.tensor
        def _(pe):
            give_credit(pe, st1, s_rdy, pt_rdy, pv_rdy, r_rdy, proj_rdy)
            pe.wait_ge(w_ld.handle, 16 * N_W)
            pe.wait_ge(const.handle, 8)
            with pe.Fori(0, NG) as i:
                pe.wait_ge(h_act.handle, h_act.at(i, 0))
                for j in range(10):
                    c = j % 2
                    if j >= 4 and j < 8:
                        pe.wait_ge(ev1.handle, ev1.at(i, j - 3))
                    elif j >= 8:
                        pe.wait_ge(ev1.handle, ev1.at(i, j - 3))
                    if j < 4:
                        if j == 0:
                            pe.wait_ge(xn_rdy.handle, xn_rdy.at(i, 1))
                        if j == 2:
                            pe.wait_ge(c_ld.handle, c_ld.at(i, 1))
                        src = (xn, cg)[j // 2]
                        for b in range(G):
                            ins = pe.transpose(bank[j][:, b * P:(b + 1) * P], src[:, b, c * P:(c + 1) * P], ident[:])
                    elif j < 8:
                        if j == 4:
                            pe.wait_ge(ev1.handle, ev1.at(i, 2))
                        if j == 6:
                            pe.wait_ge(ev1.handle, ev1.at(i, 4))
                        w, src = (wq, xT) if j < 6 else (wkv, cT)
                        for k in range(KC):
                            ins = pe.matmul(bank[j % 4], w[:, k, c * P:(c + 1) * P], src[:, k], start=(k == 0), stop=(k == KC - 1))
                    else:
                        for b in range(2 * (j - 8), 2 * (j - 8) + 2):
                            o = bank[j % 4][:, (b % 2) * D:(b % 2 + 1) * D]
                            for k in range(KC):
                                ins = pe.matmul(o, cT[:, k, b * P:(b + 1) * P], wkv[:, k, D:2 * D], start=(k == 0), stop=(k == KC - 1))
                    ins.then_inc(st1.handle, 1)

                def scores(u):
                    b, c = u // KC, u % KC
                    if u < 2:
                        pe.wait_ge(v_rdy.handle, v_rdy.at(i, 2))
                        pe.wait_ge(ev1.handle, ev1.at(i, 8))
                    if u >= 2:
                        pe.wait_ge(sm_rdy.handle, sm_rdy.at(i, u - 1))
                    pe.wait_ge(kbd_rdy.handle, kbd_rdy.at(i, u + 1))
                    for j in range(2):
                        ins = pe.matmul(psS[:, u % 2, 4 * j:4 * j + 4], qT[:, c, b * P:(b + 1) * P], kbd[:, u % 2, 4 * j:4 * j + 4],
                                        start=True, stop=True)
                    ins.then_inc(s_rdy.handle, 1)

                def probs_transposed(u):
                    pe.wait_ge(p_rdy.handle, p_rdy.at(i, u + 1))
                    for j in range(2):
                        pe.wait_ge((ptd, pta)[j].handle, (ptd, pta)[j].at(i, u))
                        for h in range(4):
                            ins = pe.transpose(psP[:, j, h * P:(h + 1) * P], s[:, u % 3, 4 * j + h], ident[:])
                        ins.then_inc(pt_rdy.handle, 1)

                def attention_out(u):
                    b, c = u // KC, u % KC
                    pe.wait_ge(vbd_rdy.handle, vbd_rdy.at(i, u + 1))
                    if c == 0:
                        pe.wait_ge(a_rdy.handle, a_rdy.at(i, b))
                    for j in range(2):
                        pe.wait_ge((ptd, pta)[j].handle, (ptd, pta)[j].at(i, u + 1))
                        for h in range(4):
                            hh = 4 * j + h
                            ins = pe.matmul(psA[:, c], vbd[:, b % 2, c * HC + hh], pT[:, u % 2, j, h * P:(h + 1) * P],
                                            start=(hh == 0), stop=(hh == HC - 1))
                    ins.then_inc(pv_rdy.handle, 1)
                    if c == 1:
                        pe.wait_ge(rz_rdy.handle, rz_rdy.at(i, u + 1))
                        for k in range(KC):
                            ins = pe.transpose(psA[:, 2 + k], rz[:, k].rearrange("p h d -> p (h d)"), ident[:])
                        ins.then_inc(r_rdy.handle, 1)

                def project(b):
                    pe.wait_ge(a_rdy.handle, a_rdy.at(i, b + 1))
                    pe.wait_ge(x1_rdy.handle, x1_rdy.at(i, b))
                    if b == 0:
                        pe.wait_ge(yb_ev.handle, yb_ev.at(i, 0))
                    for k in range(KC):
                        ins = pe.matmul(psW[:, 0:D], aT[:, k], wp[:, k], start=(k == 0), stop=(k == KC - 1))
                    ins.then_inc(proj_rdy.handle, 1)

                pe.wait_ge(y_add.handle, y_add.at(i, 0))
                scores(0)
                for u in range(UNITS):
                    if u + 1 < UNITS:
                        scores(u + 1)
                    probs_transposed(u)
                    if u >= 2 and u % 2 == 0:
                        project(u // 2 - 1)
                    attention_out(u)
                project(G - 1)

                pe.wait_ge(xn2_rdy.handle, xn2_rdy.at(i, 1))
                for c in range(KC):
                    for b in range(G):
                        ins = pe.transpose(bank[c][:, b * P:(b + 1) * P], xn2[:, b, c * P:(c + 1) * P], ident[:])
                    ins.then_inc(t2_rdy.handle, 1)
                pe.wait_ge(t2_ev.handle, t2_ev.at(i, KC))
                for b in range(G):
                    for k in range(KC):
                        ins = pe.matmul(psW[:, b * E:(b + 1) * E], x2T[:, k, b * P:(b + 1) * P], wg[:, k], start=(k == 0), stop=(k == KC - 1))
                ins.then_inc(lg_rdy.handle, 1)

                def hidden(e):
                    for m in range(HK):
                        n = e * HK + m
                        if n >= 4:
                            pe.wait_ge(h_act.handle, h_act.at(i, n - 3))
                        if n == 0:
                            pe.wait_ge(gt_ev.handle, gt_ev.at(i, 1))
                        for k in range(KC):
                            ins = pe.matmul(bank[n % 4], w1[:, e, k, m * P:(m + 1) * P], x2T[:, k], start=(k == 0), stop=(k == KC - 1))
                        ins.then_inc(h_rdy.handle, 1)

                def expert_out(e):
                    pe.wait_ge(h_act.handle, h_act.at(i, (e + 1) * HK))
                    for b in range(G):
                        n = e * G + b
                        if n >= 2:
                            pe.wait_ge(y_add.handle, y_add.at(i, n - 1))
                        for m in range(HK):
                            ins = pe.matmul(psP[:, n % 2, 0:D], hT[:, e % 2, m, b * P:(b + 1) * P], w2[:, e, m], start=(m == 0), stop=(m == HK - 1))
                        ins.then_inc(y_rdy.handle, 1)

                pe.wait_ge(gate_rdy.handle, gate_rdy.at(i, 1))
                for b in range(G):
                    ins = pe.transpose(bank[2][0:E, b * P:(b + 1) * P], gate[:, b], ident[:])
                ins.then_inc(gt_rdy.handle, 1)
                hidden(0)
                for j in range(G // 2):
                    if j:
                        pe.wait_ge(yb_ev.handle, yb_ev.at(i, j))
                    for b in range(2 * j, 2 * j + 2):
                        ins = pe.matmul(psW[:, (b % 2) * D:(b % 2 + 1) * D], gateT[:, b], b2_e[:], start=True, stop=True)
                    ins.then_inc(yb_rdy.handle, 1)
                for e in range(E):
                    if e + 1 < E:
                        hidden(e + 1)
                    expert_out(e)


_INS = ['x', 'ctx_1024', 'mask_Bx1x1xS2_ff0', 'g_xattn', 'g_ffn', 'L0_xattn_Wq', 'L0_xattn_bq', 'L0_xattn_Wkv', 'L0_xattn_bkv',
        'L0_xattn_Wp', 'L0_xattn_bp', 'L0_ffn_Wg', 'L0_ffn_bg', 'L0_ffn_W1', 'L0_ffn_b1', 'L0_ffn_W2', 'L0_ffn_b2']


def kernel(**inputs):
    import numpy as _np
    import concourse.bacc as _bacc
    from concourse import mybir as _mybir
    from concourse.bass_utils import run_bass_kernel_spmd as _run

    nc = _bacc.Bacc("TRN2", target_bir_lowering=False, num_devices=1)
    arrays, args = {}, []
    for name in _INS:
        a = _np.ascontiguousarray(inputs[name])
        arrays[f"in_{name}"] = a
        args.append(nc.dram_tensor(f"in_{name}", a.shape, _mybir.dt.from_np(a.dtype), kind="ExternalInput").ap())
    args.append(nc.dram_tensor("out_0", inputs['x'].shape, _mybir.dt.float32, kind="ExternalOutput").ap())
    gated_xattn_moe(nc, *args)
    r = _run(nc, [arrays], core_ids=[0])
    return r.results[0]["out_0"]
```

```python
from contextlib import ExitStack

import concourse.bass as bass
from concourse import mybir

F32 = mybir.dt.float32
U32 = mybir.dt.uint32
I32 = mybir.dt.int32
BF16 = mybir.dt.bfloat16
ALU = mybir.AluOpType
ACT = mybir.ActivationFunctionType
AX_X = mybir.AxisListType.X

P = 128
G = 4
NH = 16
DH = 16
HC = P // DH
KC = 2
LN_EPS = 1e-5
TEMP = 5.0
GATE_EPS = 1e-9
T = 2
TOP = 2
RING = 4
UNITS = G * KC


class Signal:

    def __init__(self, handle, per, credit, step):
        self.handle, self.per, self.credit, self.step = handle, per, credit, step

    def at(self, i, k):
        return i * (self.per * self.step) + (k + self.credit) * self.step


def gated_xattn_moe(nc, x, ctx_in, mask, g_xattn, g_ffn, Wq, bq, Wkv, bkv, Wp, bp, Wg, bg, W1, b1, W2, b2, out):
    NB, S, D = x.shape
    E, _, H = W1.shape
    NG = NB // G
    HK = H // P
    N = NB * S
    TR = T * P
    TILES = TOP * N // TR + E - 1
    LISTED = TILES + 2
    CAP = N + TR
    W = D + E + 8
    ID = D + E
    DUMMY = E * CAP
    x_rows = nc.dram_tensor("routed_rows", (E * CAP + TR, W), F32, kind="Internal").ap()
    assert S == P and D == KC * P and ctx_in.shape[1] == P and NH * DH == D

    with ExitStack() as stack:
        def sb(name, shape, dt=F32):
            return stack.enter_context(nc.sbuf_tensor(name, shape, dt))

        def ps(name, shape):
            return stack.enter_context(nc.psum_tensor(name, shape, F32))

        def part(buf, size):
            return buf.rearrange("p a b c -> p (a b c)")[:, 0:size]

        def signal(name, per=1, credit=0, step=1):
            return Signal(stack.enter_context(nc.semaphore(name)), per, credit, step)

        def give_credit(eng, *signals):
            for sig in signals:
                eng.sem_inc(sig.handle, sig.credit * sig.step)

        wq = sb("wq", [P, KC, D])
        wkv = sb("wkv", [P, KC, 2 * D])
        wp = sb("wp", [P, KC, D])
        wg = sb("wg", [P, KC, E])
        w1 = sb("w1", [P, E, KC, H])
        w2 = sb("w2", [P, E, HK, D])
        b1c = sb("b1c", [P, E, HK])
        bqk = sb("bqk", [P, 2, KC])
        bv_row = sb("bv_row", [P, D])
        bp_row = sb("bp_row", [P, D])
        bg_row = sb("bg_row", [P, E])
        b2_e = sb("b2_e", [E, D])
        gate_in = sb("gate_in", [P, 2])
        gate_tanh = sb("gate_tanh", [P, 2])
        tbp_row = sb("tbp_row", [P, D])
        ident = sb("ident", [P, P])
        head_mask = sb("head_mask", [P, HC])
        bq4 = sb("bq4", [P, KC])
        half = sb("half", [P, G])
        expert_no = sb("expert_no", [P, E])

        xg = sb("xg", [P, G, D])
        cg = sb("cg", [P, G, D])
        mg = sb("mg", [P, G, P])
        stat = sb("stat", [P, G, 6])
        mv = sb("mv", [P, G, 2])
        var_eps = sb("var_eps", [P, G])
        rstd = sb("rstd", [P, G])
        xn = sb("xn", [P, G, D])
        xb = sb("xb", [P, G, D])
        xT = sb("xT", [P, KC, G * P])
        cT = sb("cT", [P, KC, G * P])
        qT = sb("qT", [P, KC, G * P])
        kT = sb("kT", [P, KC, G * P])
        v = sb("v", [P, G, D])
        vbd = sb("vbd", [P, 2, NH, P])
        kbd = sb("kbd", [P, 2, HC, P])
        s = sb("s", [P, 3, HC, P])
        nmax = sb("nmax", [P, 2, HC])
        z = sb("z", [P, 2, HC])
        rz = sb("rz", [P, 2, HC, DH])
        pT = sb("pT", [P, 2, 2, 4 * P])
        rzT = sb("rzT", [P, KC, P])
        aT = sb("aT", [P, KC, P])
        x1 = sb("x1", [P, G, D])
        stat2 = sb("stat2", [P, G, 6])
        mv2 = sb("mv2", [P, G, 2])
        var_eps2 = sb("var_eps2", [P, G])
        rstd2 = sb("rstd2", [P, G])
        x2T = sb("x2T", [P, KC, G * P])
        logit = sb("logit", [P, G, E])
        nlmax = sb("nlmax", [P, G])
        prob = sb("prob", [P, G, E])
        top = sb("top", [P, G, 8])
        topi = sb("topi", [P, G, 8], U32)
        topf = sb("topf", [P, G, 2])
        one1 = sb("one1", [P, G, E])
        one2 = sb("one2", [P, G, E])
        gsum = sb("gsum", [P, G])
        gateT = sb("gateT", [E, G, P])
        rows = sb("rows", [P, G, W])
        xn2 = rows[:, :, 0:D]
        gate = rows[:, :, D:D + E]
        pick = sb("pick", [P, G, E])
        pick16 = sb("pick16", [P, G, E], BF16)
        before16 = sb("before16", [P, P], BF16)
        ones16 = sb("ones16", [P, P], BF16)
        base = sb("base", [P, E])
        slot = sb("slot", [P, G, E])
        dest = sb("dest", [P, TOP, G])
        dest_no = sb("dest_no", [P, TOP, G], U32)
        token = sb("token", [P, G])
        erow = sb("erow", [P, E])
        MAXT = N // TR
        tile_edge = sb("tile_edge", [1, MAXT])
        over = sb("over", [1, E, MAXT])
        n_tiles = sb("n_tiles", [1, E])
        ends = sb("ends", [1, E])
        tile_no = sb("tile_no", [1, LISTED])
        past = sb("past", [1, LISTED, E])
        past_n = sb("past_n", [1, LISTED, E])
        t_exp = sb("t_exp", [1, LISTED])
        t_row = sb("t_row", [1, LISTED])
        pad_row = sb("pad_row", [1, E], I32)
        tile_exp = sb("tile_exp", [1, LISTED], I32)
        tile_row = sb("tile_row", [1, LISTED], I32)
        pad_rows = sb("pad_rows", [P, T, W])
        pad_id = sb("pad_id", [P, T])
        xt = part(s[:], RING * T * W).rearrange("p (r a w) -> p r a w", r=RING, a=T)
        xeT = sb("xeT", [P, 2, KC, TR])
        w1s = part(vbd[:], 2 * KC * H).rearrange("p (s c n) -> p s c n", s=2, c=KC)
        b1s = sb("b1s", [P, 2, HK])
        hT = part(kbd[:], 2 * HK * TR).rearrange("p (s m n) -> p s m n", s=2, m=HK)
        y = sb("y", [P, 2, T, D])

        psS = ps("psS", [P, 2, HC, P])
        psP = ps("psP", [P, 2, 4 * P])
        psA = ps("psA", [P, 4, P])
        psW = ps("psW", [P, 512])
        bank = [psS[:, j // 2, 4 * (j % 2):4 * (j % 2) + 4, :].rearrange("p h k -> p (h k)") for j in range(4)]

        w_ld = signal("w_ld")
        mask_set = signal("mask_set")
        const = signal("const")
        dconst = signal("dconst")
        tanh_rdy = signal("tanh_rdy")
        x_ld = signal("x_ld", step=16)
        c_ld = signal("c_ld", step=16)
        m_ld = signal("m_ld", step=16)
        mv_rdy = signal("mv_rdy")
        rstd_rdy = signal("rstd_rdy", 1)
        xn_rdy = signal("xn_rdy", 1, credit=1)
        xb_rdy = signal("xb_rdy", 1, credit=1)
        st1 = signal("st1", 10, credit=1)
        ev1 = signal("ev1", 8)
        v_rdy = signal("v_rdy", 2)
        kbd_rdy = signal("kbd_rdy", UNITS)
        vbd_rdy = signal("vbd_rdy", UNITS, credit=1)
        s_rdy = signal("s_rdy", UNITS, credit=2)
        sm_rdy = signal("sm_rdy", UNITS, credit=1)
        mx_rdy = signal("mx_rdy", UNITS)
        p_rdy = signal("p_rdy", UNITS, credit=2)
        rz_rdy = signal("rz_rdy", UNITS, credit=2)
        pt_rdy = signal("pt_rdy", 2 * UNITS, credit=5)
        ptd = signal("ptd", UNITS, credit=1)
        pta = signal("pta", UNITS, credit=1)
        pv_rdy = signal("pv_rdy", UNITS, credit=4)
        r_rdy = signal("r_rdy", G, credit=1)
        r_ev = signal("r_ev", G)
        a_rdy = signal("a_rdy", G, credit=1)
        proj_rdy = signal("proj_rdy", G, credit=1)
        x1_rdy = signal("x1_rdy", G, credit=1)
        mv2_rdy = signal("mv2_rdy")
        rstd2_rdy = signal("rstd2_rdy")
        xn2_rdy = signal("xn2_rdy")
        t2_rdy = signal("t2_rdy", KC)
        t2_ev = signal("t2_ev", KC)
        lg_rdy = signal("lg_rdy")
        lm_rdy = signal("lm_rdy")
        ex_rdy = signal("ex_rdy")
        gate_rdy = signal("gate_rdy")
        gt_rdy = signal("gt_rdy")
        gt_ev = signal("gt_ev")
        yb_rdy = signal("yb_rdy", G // 2)
        yb_ev = signal("yb_ev", G // 2, credit=1)
        pick_rdy = signal("pick_rdy")
        rank_rdy = signal("rank_rdy")
        dest_rdy = signal("dest_rdy", credit=1)
        scattered = signal("scattered", TOP * G, credit=1, step=16)
        table_rdy = signal("table_rdy")
        pads_set = signal("pads_set")
        pads_stored = signal("pads_stored")
        xt_ld = [signal(f"xt_ld{k}", step=16) for k in range(RING)]
        tile_done = signal("tile_done", credit=RING)
        w1s_rdy = signal("w1s_rdy")
        xe_rdy = signal("xe_rdy")
        xe_ev = signal("xe_ev", credit=1)
        h_rdy = signal("h_rdy", 2)
        h_act = signal("h_act", 2, credit=4)
        y_rdy = signal("y_rdy", credit=2)
        y_ev = signal("y_ev", credit=2)
        added = signal("added", T, step=16)
        stored = signal("stored", credit=1, step=16)
        act_step = signal("act_step")
        passed = signal("passed")
        setup = signal("setup")
        pool_step = signal("pool_step", 2)

        xr = x.rearrange("(n g) s d -> n s g d", g=G)
        cr = ctx_in.rearrange("(n g) s d -> n s g d", g=G)
        outr = out[0:N].rearrange("(n g s) d -> n s g d", g=G, s=S)
        mr = mask.rearrange("(n g) a b k -> n (a b) (g k)", g=G)

        block = stack.enter_context(nc.Block())

        def strided(ap, n, step, m):
            w = ap.shape[-1]
            assert (n - 1) * step + m <= w
            return bass.AP(ap.tensor, ap.offset, [ap.ap[0], [step, n], [1, m]])

        N_W = 17

        def pass_gate(eng):
            eng.sem_inc(passed.handle, 1)

        @block.sync
        def _(sp):
            loads = [
                (wq[:], Wq.rearrange("(c p) n -> p c n", p=P)),
                (wkv[:], Wkv.rearrange("(c p) n -> p c n", p=P)),
                (wp[:], Wp.rearrange("(c p) n -> p c n", p=P)),
                (wg[:], Wg.rearrange("(c p) n -> p c n", p=P)),
                (bqk[:, 0, :], bq.rearrange("(c p) -> p c", p=P)),
                (bqk[:, 1, :], bkv[0:D].rearrange("(c p) -> p c", p=P)),
                (bv_row[:], bkv[D:2 * D].rearrange("(a n) -> a n", a=1).to_broadcast([P, D])),
                (bp_row[:], bp.rearrange("(a n) -> a n", a=1).to_broadcast([P, D])),
                (bg_row[:], bg.rearrange("(a n) -> a n", a=1).to_broadcast([P, E])),
                (b2_e[:], b2),
                (gate_in[:, 0:1], g_xattn.rearrange("(a n) -> a n", a=1).to_broadcast([P, 1])),
                (gate_in[:, 1:2], g_ffn.rearrange("(a n) -> a n", a=1).to_broadcast([P, 1])),
                (b1c[:], b1.rearrange("e (c p) -> p e c", p=P)),
                (w1[:, 0:E // 2], W1[0:E // 2].rearrange("e (c p) n -> p e c n", p=P)),
                (w2[:, 0:E // 2], W2[0:E // 2].rearrange("e (c p) n -> p e c n", p=P)),
                (w1[:, E // 2:], W1[E // 2:].rearrange("e (c p) n -> p e c n", p=P)),
                (w2[:, E // 2:], W2[E // 2:].rearrange("e (c p) n -> p e c n", p=P)),
            ]
            assert len(loads) == N_W
            with nc.allow_non_contiguous_dma(reason="bias columns, once"):
                for dst, src in loads:
                    sp.dma_start(dst, src).then_inc(w_ld.handle, 16)
            with sp.Fori(0, NG) as i:
                sp.wait_ge(xb_rdy.handle, xb_rdy.at(i, 0))
                sp.wait_ge(xn_rdy.handle, xn_rdy.at(i, 0))
                sp.dma_start(xg[:], xr[i]).then_inc(x_ld.handle, 16)
                sp.wait_ge(st1.handle, st1.at(i, 0))
                sp.dma_start(cg[:], cr[i]).then_inc(c_ld.handle, 16)
                sp.wait_ge(sm_rdy.handle, sm_rdy.at(i, 0))
                sp.dma_start(mg[:].rearrange("p g k -> p (g k)"), mr[i].to_broadcast([P, G * P])).then_inc(m_ld.handle, 16)
            sp.wait_ge(table_rdy.handle, 1)
            for e in range(E):
                row = sp.value_load(pad_row[0:1, e:e + 1], min_val=0, max_val=E * CAP - TR)
                sp.dma_start(x_rows[bass.ds(row, TR), :].rearrange("(a p) w -> p a w", p=P), pad_rows[:]).then_inc(pads_stored.handle, 16)
            sp.wait_ge(scattered.handle, scattered.at(NG, 0))
            sp.wait_ge(pads_stored.handle, 16 * E)

            def load_tile(i, k):
                j = i * RING + k
                sp.wait_ge(tile_done.handle, tile_done.at(j, 1 - RING))
                row = sp.value_load(tile_row[0:1, bass.ds(j, 1)], min_val=0, max_val=DUMMY)
                sp.dma_start(xt[:, k], x_rows[bass.ds(row, TR), :].rearrange("(a p) w -> p a w", p=P)).then_inc(xt_ld[k].handle, 16)

            with sp.Fori(0, TILES // RING) as i:
                for k in range(RING):
                    load_tile(i, k)
            for k in range(TILES % RING):
                load_tile(TILES // RING, k)

        @block.gpsimd
        def _(pool):
            pool.memset(ident[:], 0.0).then_inc(const.handle, 1)
            pool.memset(head_mask[:], 1.0).then_inc(const.handle, 1)
            pool.memset(vbd[:], 0.0).then_inc(const.handle, 1)
            pool.memset(half[:], -0.5).then_inc(const.handle, 1)
            pool.iota(expert_no[:], pattern=[[1, E]], base=0, channel_multiplier=0,
                      allow_small_or_imprecise_dtypes=True).then_inc(const.handle, 1)
            pool.iota(erow[:], pattern=[[CAP, E]], base=0, channel_multiplier=0,
                      allow_small_or_imprecise_dtypes=True).then_inc(setup.handle, 1)
            pool.iota(token[:], pattern=[[P, G]], base=0, channel_multiplier=1,
                      allow_small_or_imprecise_dtypes=True).then_inc(setup.handle, 1)
            pool.iota(tile_edge[:], pattern=[[TR, MAXT]], base=0, channel_multiplier=0,
                      allow_small_or_imprecise_dtypes=True).then_inc(setup.handle, 1)
            pool.iota(tile_no[:], pattern=[[1, LISTED]], base=0, channel_multiplier=0,
                      allow_small_or_imprecise_dtypes=True).then_inc(setup.handle, 1)
            pool.memset(rows[:], 0.0).then_inc(setup.handle, 1)
            pool.memset(pad_rows[:], 0.0).then_inc(setup.handle, 1)
            pool.memset(ones16[:], 1.0).then_inc(setup.handle, 1)
            pool.memset(before16[:], 1.0).then_inc(setup.handle, 1)
            pool.wait_ge(setup.handle, 8)
            pool.affine_select(out=before16[:], in_=before16[:], compare_op=ALU.is_gt, fill=0.0, base=0,
                               pattern=[[1, P]], channel_multiplier=-1).then_inc(setup.handle, 1)
            pool.iota(pad_rows[:, :, ID].bitcast(U32), pattern=[[P, T]], base=N, channel_multiplier=1).then_inc(setup.handle, 1)
            pool.wait_ge(setup.handle, 10)
            pool.wait_ge(const.handle, 5)
            pool.affine_select(out=ident[:], in_=ident[:], compare_op=ALU.not_equal, fill=1.0, base=0,
                               pattern=[[-1, P]], channel_multiplier=1).then_inc(const.handle, 1)
            pool.affine_select(out=head_mask[:], in_=head_mask[:], compare_op=ALU.is_ge, fill=0.0, base=0,
                               pattern=[[-DH, HC]], channel_multiplier=1).then_inc(const.handle, 1)
            pool.wait_ge(const.handle, 7)
            pool.affine_select(out=head_mask[:], in_=head_mask[:], compare_op=ALU.is_ge, fill=0.0, base=DH - 1,
                               pattern=[[DH, HC]], channel_multiplier=-1).then_inc(const.handle, 1)
            pool.wait_ge(const.handle, 8)
            give_credit(pool, xb_rdy, vbd_rdy, tile_done)
            pool.dma_start(x_rows[DUMMY:DUMMY + TR, :].rearrange("(a p) w -> p a w", p=P), pad_rows[:]).then_inc(scattered.handle, 16)
            pool.dma_start(out[N:N + TR, :].rearrange("(a p) n -> p a n", p=P), pad_rows[:, :, 0:D]).then_inc(stored.handle, 16)
            pool.wait_ge(w_ld.handle, 16 * N_W)
            pool.wait_ge(tanh_rdy.handle, 1)
            pool.tensor_scalar(tbp_row[:], bp_row[:], gate_tanh[:, 0:1], None, ALU.mult).then_inc(const.handle, 1)
            pool.wait_ge(const.handle, 9)
            with pool.Fori(0, NG) as i:
                pool.wait_ge(mv_rdy.handle, mv_rdy.at(i, 1))
                pass_gate(pool)
                pool.tensor_scalar(var_eps[:], mv[:, :, 1], LN_EPS, None, ALU.add).then_inc(pool_step.handle, 1)
                pool.wait_ge(pool_step.handle, pool_step.at(i, 1))
                pool.tensor_tensor(rstd[:], var_eps[:], half[:], ALU.pow).then_inc(rstd_rdy.handle, 1)
                pool.wait_ge(x1_rdy.handle, x1_rdy.at(i, 0))
                pool.tensor_tensor(xb[:], xg[:], tbp_row[:].unsqueeze(1).to_broadcast([P, G, D]), ALU.add).then_inc(xb_rdy.handle, 1)
                for u in range(UNITS):
                    b, c = u // KC, u % KC
                    if u == 0:
                        pool.wait_ge(ev1.handle, ev1.at(i, 8))
                    pool.wait_ge(s_rdy.handle, s_rdy.at(i, u - 1))
                    pool.tensor_tensor(kbd[:, u % 2], kT[:, c, b * P:(b + 1) * P].unsqueeze(1).to_broadcast([P, HC, P]),
                                       head_mask[:].unsqueeze(2).to_broadcast([P, HC, P]), ALU.mult).then_inc(kbd_rdy.handle, 1)
                    if u == 0:
                        pool.wait_ge(v_rdy.handle, v_rdy.at(i, 2))
                    pool.wait_ge(pv_rdy.handle, pv_rdy.at(i, u - 3))
                    pass_gate(pool)
                    dst = vbd[:, b % 2, c * HC:(c + 1) * HC, :].rearrange("p h k -> p (h k)")
                    pool.tensor_copy(strided(dst, HC, P + DH, DH), v[:, b, c * P:(c + 1) * P].rearrange("p (h d) -> p h d", h=HC)
                                     ).then_inc(vbd_rdy.handle, 1)
                pool.wait_ge(mv2_rdy.handle, mv2_rdy.at(i, 1))
                pass_gate(pool)
                pool.tensor_scalar(var_eps2[:], mv2[:, :, 1], LN_EPS, None, ALU.add).then_inc(pool_step.handle, 1)
                pool.wait_ge(scattered.handle, scattered.at(i, 0))
                pool.wait_ge(pool_step.handle, pool_step.at(i, 2))
                pool.tensor_tensor(rstd2[:], var_eps2[:], half[:], ALU.pow).then_inc(rstd2_rdy.handle, 1)
                pool.wait_ge(dest_rdy.handle, dest_rdy.at(i, 1))
                pass_gate(pool)
                for k in range(TOP):
                    for b in range(G):
                        pool.indirect_dma_start(x_rows, bass.IndirectOffsetOnAxis(ap=dest_no[:, k, b:b + 1], axis=0),
                                                rows[:, b, :], None).then_inc(scattered.handle, 16)
                pool.wait_ge(yb_ev.handle, yb_ev.at(i, G // 2))
                pass_gate(pool)
                pool.dma_start(outr[i], x1[:]).then_inc(stored.handle, 16)

            pool.wait_ge(table_rdy.handle, 1)
            pool.wait_ge(stored.handle, stored.at(NG, 0))

            def add_tile(i, k):
                j = i * RING + k
                pool.wait_ge(y_ev.handle, y_ev.at(j, 1))
                pass_gate(pool)
                for a in range(T):
                    pool.indirect_dma_start(out, bass.IndirectOffsetOnAxis(ap=xt[:, k, a, ID:ID + 1].bitcast(U32), axis=0),
                                            y[:, k % 2, a, :], None, compute_op=ALU.add).then_inc(added.handle, 16)
                pool.wait_ge(added.handle, added.at(j, T))
                pool.sem_inc(tile_done.handle, 1)

            with pool.Fori(0, TILES // RING) as i:
                for k in range(RING):
                    add_tile(i, k)
            for k in range(TILES % RING):
                add_tile(TILES // RING, k)
            pool.wait_ge(stored.handle, stored.at(NG, 0))

        @block.scalar
        def _(act):
            act.wait_ge(w_ld.handle, 16 * N_W)
            act.activation(gate_tanh[:], gate_in[:], ACT.Tanh).then_inc(tanh_rdy.handle, 1)
            act.activation(bq4[:], bqk[:, 0, :], ACT.Copy, scale=0.25).then_inc(act_step.handle, 1)
            act.wait_ge(act_step.handle, 1)
            give_credit(act, p_rdy, h_act, pta)
            with act.Fori(0, NG) as i:
                for j in range(8):
                    act.wait_ge(st1.handle, st1.at(i, j + 1))
                    c = j % 2
                    if j < 4:
                        dst = (xT, cT)[j // 2]
                        act.activation(dst[:, c], bank[j % 4], ACT.Copy).then_inc(ev1.handle, 1)
                    elif j < 6:
                        act.activation(qT[:, c], bank[j % 4], ACT.Identity, bias=bq4[:, c:c + 1], scale=0.25).then_inc(ev1.handle, 1)
                    else:
                        act.activation(kT[:, c], bank[j % 4], ACT.Identity, bias=bqk[:, 1, c:c + 1]).then_inc(ev1.handle, 1)

                def second_half(u):
                    act.wait_ge(pt_rdy.handle, pt_rdy.at(i, 2 * u + 2))
                    act.wait_ge(pv_rdy.handle, pv_rdy.at(i, u - 1))
                    act.activation(pT[:, u % 2, 1], psP[:, 1], ACT.Copy).then_inc(pta.handle, 1)
                    if u % 2 == 1:
                        b = u // 2
                        act.wait_ge(r_rdy.handle, r_rdy.at(i, b + 1))
                        act.wait_ge(a_rdy.handle, a_rdy.at(i, b))
                        act.activation(rzT[:].rearrange("p c k -> p (c k)"), psA[:, 2:4].rearrange("p c k -> p (c k)"),
                                       ACT.Copy).then_inc(r_ev.handle, 1)

                for u in range(UNITS):
                    act.wait_ge(mx_rdy.handle, mx_rdy.at(i, u + 1))
                    act.wait_ge(rz_rdy.handle, rz_rdy.at(i, u - 1))
                    for h in range(HC):
                        ins = act.activation(s[:, u % 3, h], s[:, u % 3, h], ACT.Exp, bias=nmax[:, u % 2, h:h + 1],
                                             accum_out=z[:, u % 2, h:h + 1])
                    ins.then_inc(p_rdy.handle, 1)
                    if u > 0:
                        second_half(u - 1)
                second_half(UNITS - 1)
                for c in range(KC):
                    act.wait_ge(t2_rdy.handle, t2_rdy.at(i, c + 1))
                    act.activation(x2T[:, c], bank[c], ACT.Copy).then_inc(t2_ev.handle, 1)
                act.wait_ge(lm_rdy.handle, lm_rdy.at(i, 1))
                act.activation(prob[:], logit[:], ACT.Exp, scale=1.0 / TEMP).then_inc(ex_rdy.handle, 1)
                act.wait_ge(gt_rdy.handle, gt_rdy.at(i, 1))
                act.activation(gateT[:].rearrange("e g k -> e (g k)"), bank[2][0:E, :], ACT.Copy).then_inc(gt_ev.handle, 1)

            def gelu_tile(i, k):
                j = i * RING + k
                for q in range(2):
                    act.wait_ge(h_rdy.handle, h_rdy.at(j, q + 1))
                    if q == 0:
                        act.wait_ge(y_rdy.handle, y_rdy.at(j, -1))
                    for m in range(2 * q, 2 * q + 2):
                        ins = act.activation(hT[:, k % 2, m], bank[2 * (k % 2) + q][:, (m % 2) * TR:(m % 2 + 1) * TR], ACT.Gelu,
                                             bias=b1s[:, k % 2, m:m + 1])
                    ins.then_inc(h_act.handle, 1)

            with act.Fori(0, TILES // RING) as i:
                for k in range(RING):
                    gelu_tile(i, k)
            for k in range(TILES % RING):
                gelu_tile(TILES // RING, k)

        @block.vector
        def _(dve):
            give_credit(dve, xn_rdy, sm_rdy, rz_rdy, ptd, a_rdy, x1_rdy, yb_ev, dest_rdy, xe_ev, y_ev)
            dve_step = signal("dve_step")
            DVE_STEPS = 31
            steps = [0]

            def link(ins, i, alone=False):
                steps[0] += 1
                ins.then_inc(dve_step.handle, 1)
                dve.wait_ge(dve_step.handle, i * DVE_STEPS + steps[0])
                if alone:
                    pass_gate(dve)

            def mark(ins):
                steps[0] += 1
                ins.then_inc(dve_step.handle, 1)

            def fence(i):
                dve.wait_ge(dve_step.handle, i * DVE_STEPS + steps[0])

            dve.wait_ge(w_ld.handle, 16 * N_W)
            dve.wait_ge(tanh_rdy.handle, 1)
            dve.wait_ge(const.handle, 9)
            dve.wait_ge(setup.handle, 10)
            dve.tensor_copy(base[:], erow[:])
            with dve.Fori(0, NG) as i:
                dve.wait_ge(x_ld.handle, x_ld.at(i, 1))
                for b in range(G):
                    ins = dve.bn_stats(stat[:, b], xg[:, b])
                link(ins, i, alone=True)
                for b in range(G):
                    ins = dve.bn_aggr(mv[:, b], stat[:, b])
                ins.then_inc(mv_rdy.handle, 1)
                dve.wait_ge(mv_rdy.handle, mv_rdy.at(i, 1))
                dve.wait_ge(rstd_rdy.handle, rstd_rdy.at(i, 1))
                for b in range(G):
                    ins = dve.tensor_scalar(xn[:, b], xg[:, b], mv[:, b, 0:1], rstd[:, b:b + 1], ALU.subtract, ALU.mult)
                ins.then_inc(xn_rdy.handle, 1)
                for j in range(2):
                    dve.wait_ge(st1.handle, st1.at(i, 9 + j))
                    if j == 0:
                        dve.wait_ge(vbd_rdy.handle, vbd_rdy.at(i, 0))
                    dve.tensor_tensor(v[:, 2 * j:2 * j + 2], bank[j].rearrange("p (b n) -> p b n", b=2),
                                      bv_row[:].unsqueeze(1).to_broadcast([P, 2, D]), ALU.add).then_inc(v_rdy.handle, 1)
                dve.wait_ge(m_ld.handle, m_ld.at(i, 1))

                def row_max(u):
                    b = u // KC
                    dve.wait_ge(s_rdy.handle, s_rdy.at(i, u + 1))
                    dve.wait_ge(pt_rdy.handle, pt_rdy.at(i, 2 * u - 4))
                    dve.tensor_tensor(s[:, u % 3], psS[:, u % 2], mg[:, b].unsqueeze(1).to_broadcast([P, HC, P]),
                                      ALU.add).then_inc(sm_rdy.handle, 1)
                    dve.wait_ge(sm_rdy.handle, sm_rdy.at(i, u + 1))
                    dve.wait_ge(p_rdy.handle, p_rdy.at(i, u - 1))
                    dve.tensor_reduce(nmax[:, u % 2], s[:, u % 3], AX_X, ALU.max, negate=True).then_inc(mx_rdy.handle, 1)

                def residual(b):
                    dve.wait_ge(proj_rdy.handle, proj_rdy.at(i, b + 1))
                    if b == 0:
                        dve.wait_ge(xb_rdy.handle, xb_rdy.at(i, 1))
                        dve.wait_ge(stored.handle, stored.at(i, 0))
                    dve.scalar_tensor_tensor(x1[:, b], psW[:, 0:D], gate_tanh[:, 0:1], xb[:, b], ALU.mult, ALU.add
                                             ).then_inc(x1_rdy.handle, 1)

                def first_half(u):
                    dve.wait_ge(p_rdy.handle, p_rdy.at(i, u + 1))
                    dve.wait_ge(r_rdy.handle, r_rdy.at(i, u // 2))
                    dve.reciprocal(rz[:, u % 2], z[:, u % 2].unsqueeze(2).to_broadcast([P, HC, DH])).then_inc(rz_rdy.handle, 1)
                    dve.wait_ge(pt_rdy.handle, pt_rdy.at(i, 2 * u + 1))
                    dve.wait_ge(pv_rdy.handle, pv_rdy.at(i, u - 1))
                    dve.tensor_copy(pT[:, u % 2, 0], psP[:, 0]).then_inc(ptd.handle, 1)

                def normalize(b):
                    dve.wait_ge(pv_rdy.handle, pv_rdy.at(i, 2 * b + 2))
                    dve.wait_ge(r_ev.handle, r_ev.at(i, b + 1))
                    dve.wait_ge(proj_rdy.handle, proj_rdy.at(i, b))
                    dve.tensor_tensor(aT[:], psA[:, 0:2], rzT[:], ALU.mult).then_inc(a_rdy.handle, 1)

                row_max(0)
                for u in range(UNITS):
                    if u + 1 < UNITS:
                        row_max(u + 1)
                    first_half(u)
                    if u >= 2 and u % 2 == 0:
                        normalize(u // 2 - 1)
                    if u >= 3 and u % 2 == 1:
                        residual(u // 2 - 1)
                normalize(G - 1)
                residual(G - 1)
                dve.wait_ge(x1_rdy.handle, x1_rdy.at(i, G))
                for b in range(G):
                    ins = dve.bn_stats(stat2[:, b], x1[:, b])
                link(ins, i, alone=True)
                for b in range(G):
                    ins = dve.bn_aggr(mv2[:, b], stat2[:, b])
                ins.then_inc(mv2_rdy.handle, 1)
                dve.wait_ge(mv2_rdy.handle, mv2_rdy.at(i, 1))
                dve.wait_ge(rstd2_rdy.handle, rstd2_rdy.at(i, 1))
                for b in range(G):
                    ins = dve.tensor_scalar(xn2[:, b], x1[:, b], mv2[:, b, 0:1], rstd2[:, b:b + 1], ALU.subtract, ALU.mult)
                ins.then_inc(xn2_rdy.handle, 1)
                link(dve.tensor_copy(rows[:, :, ID].bitcast(U32), token[:]), i)
                mark(dve.tensor_scalar(token[:], token[:], float(G * P), None, ALU.add))
                dve.wait_ge(lg_rdy.handle, lg_rdy.at(i, 1))
                link(dve.tensor_tensor(logit[:], psW[:, 0:G * E].rearrange("p (g e) -> p g e", g=G),
                                       bg_row[:].unsqueeze(1).to_broadcast([P, G, E]), ALU.add), i)
                link(dve.tensor_reduce(nlmax[:], logit[:], AX_X, ALU.max), i)
                dve.tensor_tensor(logit[:], logit[:], nlmax[:].unsqueeze(2).to_broadcast([P, G, E]), ALU.subtract
                                  ).then_inc(lm_rdy.handle, 1)
                dve.wait_ge(ex_rdy.handle, ex_rdy.at(i, 1))
                pass_gate(dve)
                for b in range(G):
                    link(dve.max(top[:, b], prob[:, b]), i, alone=True)
                    mark(dve.max_index(topi[:, b], top[:, b], prob[:, b]))
                fence(i)
                link(dve.tensor_copy(topf[:], topi[:, :, 0:2]), i)
                mark(dve.tensor_tensor(gsum[:], top[:, :, 0], top[:, :, 1], ALU.add))
                mark(dve.tensor_tensor(one1[:], expert_no[:].unsqueeze(1).to_broadcast([P, G, E]),
                                       topf[:, :, 0:1].to_broadcast([P, G, E]), ALU.is_equal))
                link(dve.tensor_tensor(one2[:], expert_no[:].unsqueeze(1).to_broadcast([P, G, E]),
                                       topf[:, :, 1:2].to_broadcast([P, G, E]), ALU.is_equal), i)
                dve.tensor_tensor(pick16[:], one1[:], one2[:], ALU.add).then_inc(pick_rdy.handle, 1)
                mark(dve.tensor_tensor(slot[:], one1[:], top[:, :, 0:1].to_broadcast([P, G, E]), ALU.mult))
                link(dve.tensor_tensor(pick[:], one2[:], top[:, :, 1:2].to_broadcast([P, G, E]), ALU.mult), i)
                mark(dve.tensor_tensor(gate, slot[:], pick[:], ALU.add))
                link(dve.tensor_reduce(nlmax[:], prob[:], AX_X, ALU.add), i)
                link(dve.scalar_tensor_tensor(gsum[:], nlmax[:], GATE_EPS, gsum[:], ALU.mult, ALU.add), i)
                link(dve.reciprocal(nlmax[:], gsum[:]), i)
                link(dve.tensor_scalar(nlmax[:], nlmax[:], gate_tanh[:, 1:2], None, ALU.mult), i)
                dve.tensor_tensor(gate, gate, nlmax[:].unsqueeze(2).to_broadcast([P, G, E]), ALU.mult
                                  ).then_inc(gate_rdy.handle, 1)
                dve.wait_ge(rank_rdy.handle, rank_rdy.at(i, 1))
                link(dve.tensor_tensor(slot[:], bank[3][:, 0:G * E].rearrange("p (g e) -> p g e", g=G),
                                       base[:].unsqueeze(1).to_broadcast([P, G, E]), ALU.add), i)
                link(dve.tensor_tensor(base[:], base[:], bank[3][:, G * E:(G + 1) * E], ALU.add), i)
                for k, one in enumerate((one1, one2)):
                    link(dve.tensor_tensor(one[:], one[:], slot[:], ALU.mult), i)
                    link(dve.tensor_reduce(dest[:, k], one[:], AX_X, ALU.add), i)
                dve.tensor_copy(dest_no[:], dest[:]).then_inc(dest_rdy.handle, 1)
                for j in range(G // 2):
                    dve.wait_ge(yb_rdy.handle, yb_rdy.at(i, j + 1))
                    dve.tensor_tensor(x1[:, 2 * j:2 * j + 2], x1[:, 2 * j:2 * j + 2], psW[:].rearrange("p (b n) -> p b n", b=2), ALU.add
                                      ).then_inc(yb_ev.handle, 1)
                dve.wait_ge(yb_ev.handle, yb_ev.at(i, G // 2))
            per_loop = steps[0]

            def chain(ins):
                steps[0] += 1
                ins.then_inc(dve_step.handle, 1)
                dve.wait_ge(dve_step.handle, NG * DVE_STEPS + steps[0] - per_loop)

            chain(dve.tensor_tensor(ends[:], base[0:1], erow[0:1], ALU.subtract))
            chain(dve.tensor_tensor(over[:], ends[:].unsqueeze(2).to_broadcast([1, E, MAXT]),
                                    tile_edge[:].unsqueeze(1).to_broadcast([1, E, MAXT]), ALU.is_gt))
            chain(dve.tensor_reduce(n_tiles[:], over[:], AX_X, ALU.add))
            chain(dve.tensor_copy(ends[:], n_tiles[:]))
            for e in range(1, E):
                chain(dve.tensor_tensor(ends[:, e:e + 1], ends[:, e:e + 1], ends[:, e - 1:e], ALU.add))
            chain(dve.tensor_tensor(past[:], tile_no[:].unsqueeze(2).to_broadcast([1, LISTED, E]),
                                    ends[:].unsqueeze(1).to_broadcast([1, LISTED, E]), ALU.is_ge))
            chain(dve.tensor_tensor(past_n[:], past[:], n_tiles[:].unsqueeze(1).to_broadcast([1, LISTED, E]), ALU.mult))
            chain(dve.tensor_reduce(t_exp[:], past[:], AX_X, ALU.add))
            chain(dve.tensor_reduce(t_row[:], past_n[:], AX_X, ALU.add))
            chain(dve.tensor_tensor(t_row[:], tile_no[:], t_row[:], ALU.subtract))
            chain(dve.tensor_scalar(t_row[:], t_row[:], float(TR), None, ALU.mult))
            chain(dve.scalar_tensor_tensor(t_row[:], t_exp[:], float(CAP), t_row[:], ALU.mult, ALU.add))
            chain(dve.tensor_scalar(t_row[:], t_row[:], float(DUMMY), None, ALU.min))
            chain(dve.tensor_scalar(t_exp[:], t_exp[:], float(E - 1), None, ALU.min))
            chain(dve.tensor_copy(tile_row[:], t_row[:]))
            chain(dve.tensor_copy(tile_exp[:], t_exp[:]))
            dve.tensor_copy(pad_row[:], base[0:1]).then_inc(table_rdy.handle, 1)

            def x_out(i, k):
                j = i * RING + k
                dve.wait_ge(xe_rdy.handle, xe_rdy.at(j, 1))
                dve.tensor_copy(xeT[:, k % 2].rearrange("p c n -> p (c n)"), psW[:]).then_inc(xe_ev.handle, 1)

            def first_weights(j, s):
                e = dve.value_load(tile_exp[0:1, bass.ds(j, 1)], min_val=0, max_val=E - 1)
                dve.wait_ge(h_act.handle, h_act.at(j, -2))
                dve.tensor_copy(b1s[:, s], b1c[:, bass.ds(e, 1), :].rearrange("p e m -> p (e m)"))
                dve.tensor_copy(w1s[:, s].rearrange("p c n -> p (c n)"), w1[:, bass.ds(e, 1)].rearrange("p e c n -> p (e c n)")
                                ).then_inc(w1s_rdy.handle, 1)

            def y_out(i, k):
                j = i * RING + k
                e = dve.value_load(tile_exp[0:1, bass.ds(j, 1)], min_val=0, max_val=E - 1)
                dve.wait_ge(y_rdy.handle, y_rdy.at(j, 1))
                dve.wait_ge(tile_done.handle, tile_done.at(j, -1))
                for a in range(T):
                    ins = dve.tensor_scalar(y[:, k % 2, a], psP[:, k % 2, a * D:(a + 1) * D], xt[:, k, a, bass.ds(e + D, 1)], None, ALU.mult)
                ins.then_inc(y_ev.handle, 1)

            first_weights(0, 0)
            x_out(0, 0)
            first_weights(1, 1)
            x_out(0, 1)
            with dve.Fori(0, TILES // RING) as i:
                for k in range(RING):
                    x_out(i + (k + 2) // RING, (k + 2) % RING)
                    first_weights(i * RING + k + 2, k % 2)
                    y_out(i, k)
            for k in range(TILES % RING):
                if k + 2 < TILES % RING:
                    x_out(TILES // RING, k + 2)
                    first_weights(TILES - TILES % RING + k + 2, k)
                y_out(TILES // RING, k)
            assert per_loop == DVE_STEPS, per_loop

        @block.tensor
        def _(pe):
            give_credit(pe, st1, s_rdy, pt_rdy, pv_rdy, r_rdy, proj_rdy, y_rdy)
            pe.wait_ge(w_ld.handle, 16 * N_W)
            pe.wait_ge(const.handle, 8)
            with pe.Fori(0, NG) as i:
                pe.wait_ge(dest_rdy.handle, dest_rdy.at(i, 0))
                for j in range(10):
                    c = j % 2
                    if j >= 4 and j < 8:
                        pe.wait_ge(ev1.handle, ev1.at(i, j - 3))
                    elif j >= 8:
                        pe.wait_ge(ev1.handle, ev1.at(i, j - 3))
                    if j < 4:
                        if j == 0:
                            pe.wait_ge(xn_rdy.handle, xn_rdy.at(i, 1))
                        if j == 2:
                            pe.wait_ge(c_ld.handle, c_ld.at(i, 1))
                        src = (xn, cg)[j // 2]
                        for b in range(G):
                            ins = pe.transpose(bank[j][:, b * P:(b + 1) * P], src[:, b, c * P:(c + 1) * P], ident[:])
                    elif j < 8:
                        if j == 4:
                            pe.wait_ge(ev1.handle, ev1.at(i, 2))
                        if j == 6:
                            pe.wait_ge(ev1.handle, ev1.at(i, 4))
                        w, src = (wq, xT) if j < 6 else (wkv, cT)
                        for k in range(KC):
                            ins = pe.matmul(bank[j % 4], w[:, k, c * P:(c + 1) * P], src[:, k], start=(k == 0), stop=(k == KC - 1))
                    else:
                        for b in range(2 * (j - 8), 2 * (j - 8) + 2):
                            o = bank[j % 4][:, (b % 2) * D:(b % 2 + 1) * D]
                            for k in range(KC):
                                ins = pe.matmul(o, cT[:, k, b * P:(b + 1) * P], wkv[:, k, D:2 * D], start=(k == 0), stop=(k == KC - 1))
                    ins.then_inc(st1.handle, 1)

                def scores(u):
                    b, c = u // KC, u % KC
                    if u < 2:
                        pe.wait_ge(v_rdy.handle, v_rdy.at(i, 2))
                        pe.wait_ge(ev1.handle, ev1.at(i, 8))
                    if u >= 2:
                        pe.wait_ge(sm_rdy.handle, sm_rdy.at(i, u - 1))
                    pe.wait_ge(kbd_rdy.handle, kbd_rdy.at(i, u + 1))
                    for j in range(2):
                        ins = pe.matmul(psS[:, u % 2, 4 * j:4 * j + 4], qT[:, c, b * P:(b + 1) * P], kbd[:, u % 2, 4 * j:4 * j + 4],
                                        start=True, stop=True)
                    ins.then_inc(s_rdy.handle, 1)

                def probs_transposed(u):
                    pe.wait_ge(p_rdy.handle, p_rdy.at(i, u + 1))
                    for j in range(2):
                        pe.wait_ge((ptd, pta)[j].handle, (ptd, pta)[j].at(i, u))
                        for h in range(4):
                            ins = pe.transpose(psP[:, j, h * P:(h + 1) * P], s[:, u % 3, 4 * j + h], ident[:])
                        ins.then_inc(pt_rdy.handle, 1)

                def attention_out(u):
                    b, c = u // KC, u % KC
                    pe.wait_ge(vbd_rdy.handle, vbd_rdy.at(i, u + 1))
                    if c == 0:
                        pe.wait_ge(a_rdy.handle, a_rdy.at(i, b))
                    for j in range(2):
                        pe.wait_ge((ptd, pta)[j].handle, (ptd, pta)[j].at(i, u + 1))
                        for h in range(4):
                            hh = 4 * j + h
                            ins = pe.matmul(psA[:, c], vbd[:, b % 2, c * HC + hh], pT[:, u % 2, j, h * P:(h + 1) * P],
                                            start=(hh == 0), stop=(hh == HC - 1))
                    ins.then_inc(pv_rdy.handle, 1)
                    if c == 1:
                        pe.wait_ge(rz_rdy.handle, rz_rdy.at(i, u + 1))
                        for k in range(KC):
                            ins = pe.transpose(psA[:, 2 + k], rz[:, k].rearrange("p h d -> p (h d)"), ident[:])
                        ins.then_inc(r_rdy.handle, 1)

                def project(b):
                    pe.wait_ge(a_rdy.handle, a_rdy.at(i, b + 1))
                    pe.wait_ge(x1_rdy.handle, x1_rdy.at(i, b))
                    if b == 0:
                        pe.wait_ge(yb_ev.handle, yb_ev.at(i, 0))
                    for k in range(KC):
                        ins = pe.matmul(psW[:, 0:D], aT[:, k], wp[:, k], start=(k == 0), stop=(k == KC - 1))
                    ins.then_inc(proj_rdy.handle, 1)

                scores(0)
                scores(1)
                for u in range(UNITS):
                    probs_transposed(u)
                    if u + 2 < UNITS:
                        scores(u + 2)
                    if u >= 2 and u % 2 == 0:
                        project(u // 2 - 1)
                    attention_out(u)
                project(G - 1)

                pe.wait_ge(xn2_rdy.handle, xn2_rdy.at(i, 1))
                for c in range(KC):
                    for b in range(G):
                        ins = pe.transpose(bank[c][:, b * P:(b + 1) * P], xn2[:, b, c * P:(c + 1) * P], ident[:])
                    ins.then_inc(t2_rdy.handle, 1)
                pe.wait_ge(t2_ev.handle, t2_ev.at(i, KC))
                for b in range(G):
                    for k in range(KC):
                        ins = pe.matmul(psW[:, b * E:(b + 1) * E], x2T[:, k, b * P:(b + 1) * P], wg[:, k], start=(k == 0), stop=(k == KC - 1))
                ins.then_inc(lg_rdy.handle, 1)

                pe.wait_ge(pick_rdy.handle, pick_rdy.at(i, 1))
                pe.matmul(bank[3][:, 0:G * E], before16[:], pick16[:].rearrange("p g e -> p (g e)"), start=True, stop=False, skip_group_check=True)
                for b in range(G - 1):
                    pe.matmul(bank[3][:, (b + 1) * E:G * E].rearrange("p (g e) -> p g e", e=E), ones16[:],
                              pick16[:, b:b + 1].to_broadcast([P, G - 1 - b, E]), start=False, stop=False, skip_group_check=True)
                for b in range(G):
                    ins = pe.matmul(bank[3][:, G * E:(G + 1) * E], ones16[:], pick16[:, b], start=False, stop=(b == G - 1), skip_group_check=True)
                ins.then_inc(rank_rdy.handle, 1)

                pe.wait_ge(gate_rdy.handle, gate_rdy.at(i, 1))
                for b in range(G):
                    ins = pe.transpose(bank[2][0:E, b * P:(b + 1) * P], gate[:, b], ident[:])
                ins.then_inc(gt_rdy.handle, 1)
                pe.wait_ge(gt_ev.handle, gt_ev.at(i, 1))
                for j in range(G // 2):
                    if j:
                        pe.wait_ge(yb_ev.handle, yb_ev.at(i, j))
                    for b in range(2 * j, 2 * j + 2):
                        ins = pe.matmul(psW[:, (b % 2) * D:(b % 2 + 1) * D], gateT[:, b], b2_e[:], start=True, stop=True)
                    ins.then_inc(yb_rdy.handle, 1)

            def tile_transposed(i, k):
                j = i * RING + k
                pe.wait_ge(xt_ld[k].handle, xt_ld[k].at(i, 1))
                pe.wait_ge(xe_ev.handle, xe_ev.at(j, 0))
                for c in range(KC):
                    for a in range(T):
                        ins = pe.transpose(psW[:, (c * T + a) * P:(c * T + a + 1) * P], xt[:, k, a, c * P:(c + 1) * P], ident[:])
                ins.then_inc(xe_rdy.handle, 1)

            def hidden(i, k):
                j = i * RING + k
                pe.wait_ge(xe_ev.handle, xe_ev.at(j, 1))
                pe.wait_ge(w1s_rdy.handle, w1s_rdy.at(j, 1))
                for q in range(2):
                    pe.wait_ge(h_act.handle, h_act.at(j, q - 3))
                    for m in range(2 * q, 2 * q + 2):
                        for c in range(KC):
                            ins = pe.matmul(bank[2 * (k % 2) + q][:, (m % 2) * TR:(m % 2 + 1) * TR], w1s[:, k % 2, c, m * P:(m + 1) * P],
                                            xeT[:, k % 2, c], start=(c == 0), stop=(c == KC - 1))
                    ins.then_inc(h_rdy.handle, 1)

            def expert_out(i, k):
                j = i * RING + k
                e = pe.value_load(tile_exp[0:1, bass.ds(j, 1)], min_val=0, max_val=E - 1)
                pe.wait_ge(h_act.handle, h_act.at(j, 2))
                pe.wait_ge(y_ev.handle, y_ev.at(j, -1))
                for a in range(T):
                    for m in range(HK):
                        ins = pe.matmul(psP[:, k % 2, a * D:(a + 1) * D], hT[:, k % 2, m, a * P:(a + 1) * P],
                                        w2[:, bass.ds(e, 1), m].rearrange("p e n -> p (e n)"), start=(m == 0), stop=(m == HK - 1))
                ins.then_inc(y_rdy.handle, 1)

            pe.wait_ge(yb_ev.handle, yb_ev.at(NG, 0))
            pe.wait_ge(table_rdy.handle, 1)
            tile_transposed(0, 0)
            hidden(0, 0)
            tile_transposed(0, 1)
            with pe.Fori(0, TILES // RING) as i:
                for k in range(RING):
                    hidden(i + (k + 1) // RING, (k + 1) % RING)
                    tile_transposed(i + (k + 2) // RING, (k + 2) % RING)
                    expert_out(i, k)
            for k in range(TILES % RING):
                if k + 1 < TILES % RING:
                    hidden(TILES // RING, k + 1)
                if k + 2 < TILES % RING:
                    tile_transposed(TILES // RING, k + 2)
                expert_out(TILES // RING, k)


_INS = ['x', 'ctx_1024', 'mask_Bx1x1xS2_ff0', 'g_xattn', 'g_ffn', 'L0_xattn_Wq', 'L0_xattn_bq', 'L0_xattn_Wkv', 'L0_xattn_bkv',
        'L0_xattn_Wp', 'L0_xattn_bp', 'L0_ffn_Wg', 'L0_ffn_bg', 'L0_ffn_W1', 'L0_ffn_b1', 'L0_ffn_W2', 'L0_ffn_b2']


def kernel(**inputs):
    import numpy as _np
    import concourse.bacc as _bacc
    from concourse import mybir as _mybir
    from concourse.bass_utils import run_bass_kernel_spmd as _run

    nc = _bacc.Bacc("TRN2", target_bir_lowering=False, num_devices=1)
    arrays, args = {}, []
    for name in _INS:
        a = _np.ascontiguousarray(inputs[name])
        arrays[f"in_{name}"] = a
        args.append(nc.dram_tensor(f"in_{name}", a.shape, _mybir.dt.from_np(a.dtype), kind="ExternalInput").ap())
    nb, s, d = inputs['x'].shape
    args.append(nc.dram_tensor("out_0", (nb * s + T * P, d), _mybir.dt.float32, kind="ExternalOutput").ap())
    gated_xattn_moe(nc, *args)
    r = _run(nc, [arrays], core_ids=[0])
    return r.results[0]["out_0"][0:nb * s].reshape(nb, s, d)
```

```python
from contextlib import ExitStack

import concourse.bass as bass
from concourse import mybir

F32 = mybir.dt.float32
U32 = mybir.dt.uint32
I32 = mybir.dt.int32
BF16 = mybir.dt.bfloat16
F32R = mybir.dt.float32r
ALU = mybir.AluOpType
ACT = mybir.ActivationFunctionType
AX_X = mybir.AxisListType.X

P = 128
G = 4
NH = 16
DH = 16
HC = P // DH
KC = 2
LN_EPS = 1e-5
TEMP = 5.0
GATE_EPS = 1e-9
T = 2
TOP = 2
RING = 6
DVE_UNITS = 4
UNITS = G * KC


class Signal:

    def __init__(self, handle, per, credit, step):
        self.handle, self.per, self.credit, self.step = handle, per, credit, step

    def at(self, i, k):
        value = i * (self.per * self.step) + (k + self.credit) * self.step
        assert not isinstance(value, int) or value > 0, (self.handle, i, k)
        return value


def gated_xattn_moe(nc, x, ctx_in, mask, g_xattn, g_ffn, Wq, bq, Wkv, bkv, Wp, bp, Wg, bg, W1, b1, W2, b2, out):
    NB, S, D = x.shape
    E, _, H = W1.shape
    NG = NB // G
    HK = H // P
    N = NB * S
    TR = T * P
    TILES = TOP * N // TR + E - 1
    LISTED = TILES + 2
    CAP = N + TR
    W = D + E + 8
    ID = D + E
    DUMMY = E * CAP
    x_rows = nc.dram_tensor("routed_rows", (E * CAP + TR, W), F32, kind="Internal").ap()
    assert TILES % RING >= 2 and S == P and D == KC * P and ctx_in.shape[1] == P and NH * DH == D

    with ExitStack() as stack:
        def sb(name, shape, dt=F32):
            return stack.enter_context(nc.sbuf_tensor(name, shape, dt))

        def ps(name, shape):
            return stack.enter_context(nc.psum_tensor(name, shape, F32))

        def signal(name, per=1, credit=0, step=1):
            return Signal(stack.enter_context(nc.semaphore(name)), per, credit, step)

        def give_credit(eng, *signals):
            for sig in signals:
                eng.sem_inc(sig.handle, sig.credit * sig.step)

        def scoped(scope, name, shape, dt=F32):
            return scope.enter_context(nc.sbuf_tensor(name, shape, dt))

        with ExitStack() as loaded:
            w1 = scoped(loaded, "w1", [P, E, KC, H])
            w2 = scoped(loaded, "w2", [P, E, HK, D])
        w1_lo = sb("w1_lo", [P, E, KC, H], F32R)
        w2_lo = sb("w2_lo", [P, E, HK, D], F32R)

        wg = sb("wg", [P, KC, E])
        b1c = sb("b1c", [P, E, HK])
        bqk = sb("bqk", [P, 2, KC])
        bg_row = sb("bg_row", [P, E])
        b2_row = sb("b2_row", [P, E, D])
        gate_in = sb("gate_in", [P, 2])
        gate_tanh = sb("gate_tanh", [P, 2])
        ident = sb("ident", [P, P])
        head_mask = sb("head_mask", [P, HC])
        bq4 = sb("bq4", [P, KC])
        half = sb("half", [P, G])
        expert_no = sb("expert_no", [P, E])

        stat = sb("stat", [P, G, 6])
        mv = sb("mv", [P, G, 2])
        var_eps = sb("var_eps", [P, G])
        rstd = sb("rstd", [P, G])
        s_space = sb("s_space", [P, max(2 * HC * P, RING * T * W)])
        s = s_space[:, 0:2 * HC * P].rearrange("p (r h k) -> p r h k", r=2, h=HC)
        nmax = sb("nmax", [P, 2, HC])
        z = sb("z", [P, 2, HC])
        stat2 = sb("stat2", [P, G, 6])
        mv2 = sb("mv2", [P, G, 2])
        var_eps2 = sb("var_eps2", [P, G])
        rstd2 = sb("rstd2", [P, G])
        logit = sb("logit", [P, G, E])
        nlmax = sb("nlmax", [P, G])
        prob = sb("prob", [P, G, E])
        top = sb("top", [P, G, 8])
        topi = sb("topi", [P, G, 8], U32)
        topf = sb("topf", [P, G, 2])
        one1 = sb("one1", [P, G, E])
        one2 = sb("one2", [P, G, E])
        gsum = sb("gsum", [P, G])
        pick = sb("pick", [P, G, E])
        pick16 = sb("pick16", [P, G, E], BF16)
        before16 = sb("before16", [P, P], BF16)
        ones16 = sb("ones16", [P, P], BF16)
        base = sb("base", [P, E])
        slot = sb("slot", [P, G, E])
        dest = sb("dest", [P, TOP, G])
        dest_no = sb("dest_no", [P, TOP, G], U32)
        token = sb("token", [P, G])
        erow = sb("erow", [P, E])
        MAXT = N // TR
        tile_edge = sb("tile_edge", [1, MAXT])
        n_tiles = sb("n_tiles", [1, E])
        ends = sb("ends", [1, E])
        tile_no = sb("tile_no", [1, LISTED])
        t_exp = sb("t_exp", [1, LISTED])
        t_row = sb("t_row", [1, LISTED])
        pad_row = sb("pad_row", [1, E], I32)
        tile_exp = sb("tile_exp", [1, LISTED], I32)
        tile_row = sb("tile_row", [1, LISTED], I32)
        xt = s_space[:, 0:RING * T * W].rearrange("p (r a w) -> p r a w", r=RING, a=T)

        with ExitStack() as attention_phase:
            def first(name, shape, dt=F32):
                return scoped(attention_phase, name, shape, dt)

            wq = first("wq", [P, KC, D])
            wkv = first("wkv", [P, KC, 2 * D])
            wp = first("wp", [P, KC, D])
            bv_row = first("bv_row", [P, D])
            bp_row = first("bp_row", [P, D])
            xg = first("xg", [P, G, D])
            cg = first("cg", [P, G, D])
            mg = first("mg", [P, G, P])
            xn = first("xn", [P, G, D])
            xb = first("xb", [P, G, D])
            xT = first("xT", [P, KC, G * P])
            cT = first("cT", [P, KC, G * P])
            q_f = first("q_f", [P, G * P])
            k_f = first("k_f", [P, G * P])
            q_hi = first("q_hi", [P, KC, G * P], F32R)
            q_lo = first("q_lo", [P, KC, G * P], F32R)
            k_hi = first("k_hi", [P, KC, G * P], F32R)
            k_lo = first("k_lo", [P, KC, G * P], F32R)
            v = first("v", [P, G, D])
            vbd = first("vbd", [P, 2, NH, P])
            kbd = [first(f"kbd{j}", [P, 2, HC, P], F32R) for j in range(2)]
            rz8 = first("rz8", [P, 2, HC])
            rz = first("rz", [P, 2, HC, DH])
            pT = first("pT", [P, 2, 2, 4 * P])
            rzT = first("rzT", [P, KC, P])
            aT = first("aT", [P, KC, P])
            x1 = first("x1", [P, G, D])
            x2T = first("x2T", [P, KC, G * P])
            rows = first("rows", [P, G, W])
            pad_rows = first("pad_rows", [P, T, W])
        xn2 = rows[:, :, 0:D]
        gate = rows[:, :, D:D + E]

        w1_hi = sb("w1_hi", [P, E, KC, H], F32R)
        w2_hi = sb("w2_hi", [P, E, HK, D], F32R)
        with ExitStack() as between_phases:
            over = scoped(between_phases, "over", [1, E, MAXT])
            past = scoped(between_phases, "past", [1, LISTED, E])
            past_n = scoped(between_phases, "past_n", [1, LISTED, E])
        xe_hi = sb("xe_hi", [P, 2, KC, TR], F32R)
        xe_lo = sb("xe_lo", [P, 2, KC, TR], F32R)
        w1s_hi = sb("w1s_hi", [P, 2, KC, H], F32R)
        w1s_lo = sb("w1s_lo", [P, 2, KC, H], F32R)
        gelu_loaded = sb("gelu_loaded", [P, 1])
        b1s = sb("b1s", [P, 2, HK])
        hT = sb("hT", [P, HK, TR])
        h_hi = sb("h_hi", [P, 2, HK, TR], F32R)
        h_lo = sb("h_lo", [P, 2, HK, TR], F32R)
        y = sb("y", [P, 2, T, D])

        psS = ps("psS", [P, 2, HC, P])
        psP = ps("psP", [P, 2, 4 * P])
        psA = ps("psA", [P, 4, P])
        psW = ps("psW", [P, 512])
        bank = [psS[:, j // 2, 4 * (j % 2):4 * (j % 2) + 4, :].rearrange("p h k -> p (h k)") for j in range(4)]

        w_ld = signal("w_ld")
        ffn_ld = signal("ffn_ld")
        const = signal("const")
        tanh_rdy = signal("tanh_rdy")
        x_ld = signal("x_ld", step=16)
        c_ld = signal("c_ld", step=16)
        m_ld = [signal(f"m_ld{j}", step=16) for j in range(2)]
        stat_rdy = signal("stat_rdy")
        mv_rdy = signal("mv_rdy")
        rstd_rdy = signal("rstd_rdy")
        xn_rdy = signal("xn_rdy", credit=1)
        xb_rdy = signal("xb_rdy", credit=1)
        cT_rdy = signal("cT_rdy", KC, credit=1)
        cT_ev = signal("cT_ev", KC)
        xT_rdy = signal("xT_rdy", KC, credit=1)
        xT_ev = signal("xT_ev", KC)
        q_rdy = signal("q_rdy", KC)
        q_ev = signal("q_ev", KC)
        k_rdy = signal("k_rdy", KC)
        k_ev = signal("k_ev", KC)
        v_ps = signal("v_ps", 2)
        v_rdy = signal("v_rdy", 2, credit=1)
        kbd_dve = signal("kbd_dve", DVE_UNITS, credit=DVE_UNITS)
        kbd_rdy = signal("kbd_rdy", UNITS, credit=2)
        vbd_rdy = signal("vbd_rdy", UNITS, credit=5)
        s_half = signal("s_half", UNITS)
        s_rdy = signal("s_rdy", UNITS, credit=2)
        sm_rdy = signal("sm_rdy", UNITS, credit=5)
        mx_rdy = signal("mx_rdy", UNITS)
        p_rdy = signal("p_rdy", UNITS, credit=2)
        rz_rdy = signal("rz_rdy", UNITS, credit=2)
        rz_spread = signal("rz_spread", UNITS)
        q_hi_rdy = signal("q_hi_rdy", KC)
        k_hi_rdy = signal("k_hi_rdy", KC)
        q_split = signal("q_split", KC, credit=1)
        k_split = signal("k_split", KC, credit=1)
        pt_rdy = signal("pt_rdy", 2 * UNITS, credit=5)
        ptd = signal("ptd", UNITS, credit=1)
        pta = signal("pta", UNITS, credit=1)
        pv_rdy = signal("pv_rdy", UNITS, credit=4)
        r_rdy = signal("r_rdy", G, credit=1)
        r_ev = signal("r_ev", G)
        a_rdy = signal("a_rdy", G, credit=1)
        proj_rdy = signal("proj_rdy", G, credit=1)
        x1_rdy = signal("x1_rdy", G, credit=6)
        stat2_rdy = signal("stat2_rdy")
        mv2_rdy = signal("mv2_rdy")
        rstd2_rdy = signal("rstd2_rdy")
        xn2_rdy = signal("xn2_rdy", credit=1)
        t2_rdy = signal("t2_rdy", KC)
        t2_ev = signal("t2_ev", KC)
        lg_rdy = signal("lg_rdy")
        lg_ev = signal("lg_ev")
        lm_rdy = signal("lm_rdy")
        ex_rdy = signal("ex_rdy")
        pick_rdy = signal("pick_rdy")
        rank_rdy = signal("rank_rdy")
        rank_ev = signal("rank_ev")
        dest_rdy = signal("dest_rdy")
        scattered = signal("scattered", TOP * G, credit=1, step=16)
        table_rdy = signal("table_rdy")
        pads_stored = signal("pads_stored")
        xt_ld = [signal(f"xt_ld{k}", step=16) for k in range(RING)]
        tile_done = signal("tile_done", credit=RING)
        phase_a_done = signal("phase_a_done")
        hi_rdy = signal("hi_rdy")
        lo_rdy = signal("lo_rdy")
        lo_rdy_pool = signal("lo_rdy_pool")
        hi_copied = signal("hi_copied")
        lo_copied = signal("lo_copied")
        xh_rdy = signal("xh_rdy")
        h_split = signal("h_split", 2, credit=2)
        xe_rdy = signal("xe_rdy")
        xe_ev = signal("xe_ev", credit=1)
        h_rdy = signal("h_rdy", 2, credit=4)
        h_act = signal("h_act", 2, credit=4)
        y_rdy = signal("y_rdy", credit=2)
        y_ev = signal("y_ev", credit=2)
        added = signal("added", T, step=16)
        stored = signal("stored", credit=1, step=16)
        act_step = signal("act_step")
        passed = signal("passed")
        setup = signal("setup")
        eps_step = signal("eps_step")
        eps2_step = signal("eps2_step")
        y_step = signal("y_step")

        xr = x.rearrange("(n g) s d -> n s g d", g=G)
        cr = ctx_in.rearrange("(n g) s d -> n s g d", g=G)
        outr = out[0:N].rearrange("(n g s) d -> n s g d", g=G, s=S)
        mr = mask.rearrange("(n g) a b k -> n (a b) (g k)", g=G)

        block = stack.enter_context(nc.Block())

        def strided(ap, n, step, m):
            w = ap.shape[-1]
            assert (n - 1) * step + m <= w
            return bass.AP(ap.tensor, ap.offset, [ap.ap[0], [step, n], [1, m]])

        N_W, N_FFN = 11, 6

        def pipeline(eng, turn):
            turn(-1, False, False, True)
            turn(0, False, True, True)
            turn(1, True, True, True)
            with eng.Fori(2, NG - 1) as g:
                turn(g, True, True, True)
            turn(NG - 1, True, True, False)
            turn(NG, True, False, False)

        def piece(p, w):
            return w[p % 2][:, p // 2].rearrange("p c n -> p (c n)")
        POOL_PIECES = [p for p in range(2 * E) if p % 8 >= 5]
        DVE_PIECES = [p for p in range(2 * E) if p % 8 < 5]

        def pass_gate(eng):
            eng.sem_inc(passed.handle, 1)

        @block.sync
        def _(sp):
            loads = [
                (wq[:], Wq.rearrange("(c p) n -> p c n", p=P)),
                (wkv[:], Wkv.rearrange("(c p) n -> p c n", p=P)),
                (wp[:], Wp.rearrange("(c p) n -> p c n", p=P)),
                (wg[:], Wg.rearrange("(c p) n -> p c n", p=P)),
                (bqk[:, 0, :], bq.rearrange("(c p) -> p c", p=P)),
                (bqk[:, 1, :], bkv[0:D].rearrange("(c p) -> p c", p=P)),
                (bv_row[:], bkv[D:2 * D].rearrange("(a n) -> a n", a=1).to_broadcast([P, D])),
                (bp_row[:], bp.rearrange("(a n) -> a n", a=1).to_broadcast([P, D])),
                (bg_row[:], bg.rearrange("(a n) -> a n", a=1).to_broadcast([P, E])),
                (gate_in[:, 0:1], g_xattn.rearrange("(a n) -> a n", a=1).to_broadcast([P, 1])),
                (gate_in[:, 1:2], g_ffn.rearrange("(a n) -> a n", a=1).to_broadcast([P, 1])),
            ]
            assert len(loads) == N_W
            with nc.allow_non_contiguous_dma(reason="bias columns, once"):
                for dst, src in loads:
                    sp.dma_start(dst, src).then_inc(w_ld.handle, 16)

            def load_group(i):
                sp.wait_ge(cT_rdy.handle, cT_rdy.at(i, 0))
                sp.dma_start(cg[:], cr[i]).then_inc(c_ld.handle, 16)
                if not isinstance(i, int):
                    store_group(i - 2, i)
                sp.wait_ge(xn_rdy.handle, xn_rdy.at(i, 0))
                sp.wait_ge(xb_rdy.handle, xb_rdy.at(i, 0))
                sp.dma_start(xg[:], xr[i]).then_inc(x_ld.handle, 16)
                for j in range(2):
                    sp.wait_ge(sm_rdy.handle, sm_rdy.at(i, 4 * j - 4))
                    sp.dma_start(mg[:, 2 * j:2 * j + 2].rearrange("p g k -> p (g k)"),
                                 mr[i][:, 2 * j * P:(2 * j + 2) * P].to_broadcast([P, 2 * P])).then_inc(m_ld[j].handle, 16)

            def store_group(j, i):
                sp.wait_ge(x1_rdy.handle, x1_rdy.at(i, -G))
                sp.dma_start(outr[j], x1[:]).then_inc(stored.handle, 16)

            load_group(0)
            sp.wait_ge(setup.handle, 10)
            sp.dma_start(out[N:N + TR, :].rearrange("(a p) n -> p a n", p=P), pad_rows[:, :, 0:D]).then_inc(stored.handle, 16)
            load_group(1)
            with sp.Fori(2, NG) as i:
                load_group(i)
            store_group(NG - 2, NG)
            store_group(NG - 1, NG + 1)
            sp.wait_ge(table_rdy.handle, 1)
            for e in range(E):
                row = sp.value_load(pad_row[0:1, e:e + 1], min_val=0, max_val=E * CAP - TR)
                sp.dma_start(x_rows[bass.ds(row, TR), :].rearrange("(a p) w -> p a w", p=P), pad_rows[:]).then_inc(pads_stored.handle, 16)
            sp.wait_ge(scattered.handle, scattered.at(NG, 0))
            sp.wait_ge(pads_stored.handle, 16 * E)

            def load_tile(i, k):
                j = i * RING + k
                sp.wait_ge(tile_done.handle, tile_done.at(j, 1 - RING))
                row = sp.value_load(tile_row[0:1, bass.ds(j, 1)], min_val=0, max_val=DUMMY)
                sp.dma_start(xt[:, k], x_rows[bass.ds(row, TR), :].rearrange("(a p) w -> p a w", p=P)).then_inc(xt_ld[k].handle, 16)

            with sp.Fori(0, TILES // RING) as i:
                for k in range(RING):
                    load_tile(i, k)
            for k in range(TILES % RING):
                load_tile(TILES // RING, k)

        @block.gpsimd
        def _(pool):
            pool.memset(ident[:], 0.0).then_inc(const.handle, 1)
            pool.memset(head_mask[:], 1.0).then_inc(const.handle, 1)
            pool.memset(vbd[:], 0.0).then_inc(const.handle, 1)
            pool.memset(half[:], -0.5).then_inc(const.handle, 1)
            pool.iota(expert_no[:], pattern=[[1, E]], base=0, channel_multiplier=0,
                      allow_small_or_imprecise_dtypes=True).then_inc(const.handle, 1)
            pool.iota(erow[:], pattern=[[CAP, E]], base=0, channel_multiplier=0,
                      allow_small_or_imprecise_dtypes=True).then_inc(setup.handle, 1)
            pool.iota(token[:], pattern=[[P, G]], base=0, channel_multiplier=1,
                      allow_small_or_imprecise_dtypes=True).then_inc(setup.handle, 1)
            pool.iota(tile_edge[:], pattern=[[TR, MAXT]], base=0, channel_multiplier=0,
                      allow_small_or_imprecise_dtypes=True).then_inc(setup.handle, 1)
            pool.iota(tile_no[:], pattern=[[1, LISTED]], base=0, channel_multiplier=0,
                      allow_small_or_imprecise_dtypes=True).then_inc(setup.handle, 1)
            pool.memset(rows[:], 0.0).then_inc(setup.handle, 1)
            pool.memset(pad_rows[:], 0.0).then_inc(setup.handle, 1)
            pool.memset(ones16[:], 1.0).then_inc(setup.handle, 1)
            pool.memset(before16[:], 1.0).then_inc(setup.handle, 1)
            pool.wait_ge(setup.handle, 8)
            pool.affine_select(out=before16[:], in_=before16[:], compare_op=ALU.is_gt, fill=0.0, base=0,
                               pattern=[[1, P]], channel_multiplier=-1).then_inc(setup.handle, 1)
            pool.iota(pad_rows[:, :, ID].bitcast(U32), pattern=[[P, T]], base=N, channel_multiplier=1).then_inc(setup.handle, 1)
            pool.wait_ge(setup.handle, 10)
            pool.wait_ge(const.handle, 5)
            pool.affine_select(out=ident[:], in_=ident[:], compare_op=ALU.not_equal, fill=1.0, base=0,
                               pattern=[[-1, P]], channel_multiplier=1).then_inc(const.handle, 1)
            pool.affine_select(out=head_mask[:], in_=head_mask[:], compare_op=ALU.is_ge, fill=0.0, base=0,
                               pattern=[[-DH, HC]], channel_multiplier=1).then_inc(const.handle, 1)
            pool.wait_ge(const.handle, 7)
            pool.affine_select(out=head_mask[:], in_=head_mask[:], compare_op=ALU.is_ge, fill=0.0, base=DH - 1,
                               pattern=[[DH, HC]], channel_multiplier=-1).then_inc(const.handle, 1)
            pool.wait_ge(const.handle, 8)
            give_credit(pool, xb_rdy, kbd_rdy, tile_done)
            pool.dma_start(x_rows[DUMMY:DUMMY + TR, :].rearrange("(a p) w -> p a w", p=P), pad_rows[:]).then_inc(scattered.handle, 16)
            pool.wait_ge(w_ld.handle, 16 * N_W)
            pool.wait_ge(tanh_rdy.handle, 1)
            pool.tensor_scalar(bp_row[:], bp_row[:], gate_tanh[:, 0:1], None, ALU.mult).then_inc(const.handle, 1)
            pool.wait_ge(const.handle, 9)

            def keys_apart(g, n):
                b, c = n % UNITS // KC, n % KC
                if n >= UNITS and n < UNITS + KC:
                    pool.wait_ge(k_split.handle, k_split.at(g, KC + c + 1))
                pool.wait_ge(s_rdy.handle, s_rdy.at(g, n - 1))
                for j in range(2 if n % UNITS >= DVE_UNITS else 1):
                    ins = pool.tensor_tensor(kbd[j][:, n % 2], (k_hi, k_lo)[j][:, c, b * P:(b + 1) * P].unsqueeze(1).to_broadcast([P, HC, P]),
                                             head_mask[:].unsqueeze(2).to_broadcast([P, HC, P]), ALU.mult)
                ins.then_inc(kbd_rdy.handle, 1)

            def scatter(g, u):
                for kb in {6: range(0, 3), 7: range(3, 6), 0: range(6, TOP * G)}[u]:
                    k, b = kb // G, kb % G
                    pool.indirect_dma_start(x_rows, bass.IndirectOffsetOnAxis(ap=dest_no[:, k, b:b + 1], axis=0),
                                            rows[:, b, :], None).then_inc(scattered.handle, 16)

            def turn(g, has_tail, has_attention, has_next):
                for u in range(UNITS):
                    n = u + 3
                    if has_attention if n < UNITS else has_next:
                        keys_apart(g, n)
                    if u == 0 and not isinstance(g, int) or u == 0 and has_tail and g >= 2:
                        scatter(g, u)
                    if u == 0 and has_attention:
                        pool.wait_ge(x1_rdy.handle, x1_rdy.at(g, 0))
                        pool.wait_ge(x_ld.handle, x_ld.at(g, 1))
                        pool.tensor_tensor(xb[:], xg[:], bp_row[:].unsqueeze(1).to_broadcast([P, G, D]), ALU.add
                                           ).then_inc(xb_rdy.handle, 1)
                    if u == 1 and has_tail:
                        pool.wait_ge(mv2_rdy.handle, mv2_rdy.at(g, 0))
                        pass_gate(pool)
                        pool.tensor_scalar(var_eps2[:], mv2[:, :, 1], LN_EPS, None, ALU.add).then_inc(eps2_step.handle, 1)
                        pool.wait_ge(scattered.handle, scattered.at(g, -TOP * G))
                        pool.wait_ge(eps2_step.handle, eps2_step.at(g, 0))
                        pool.tensor_tensor(rstd2[:], var_eps2[:], half[:], ALU.pow).then_inc(rstd2_rdy.handle, 1)
                    if u == 2 and has_next:
                        pool.wait_ge(mv_rdy.handle, mv_rdy.at(g, 2))
                        pass_gate(pool)
                        pool.tensor_scalar(var_eps[:], mv[:, :, 1], LN_EPS, None, ALU.add).then_inc(eps_step.handle, 1)
                        pool.wait_ge(eps_step.handle, eps_step.at(g, 2))
                        pool.tensor_tensor(rstd[:], var_eps[:], half[:], ALU.pow).then_inc(rstd_rdy.handle, 1)
                    if u >= 6 and has_tail:
                        pool.wait_ge(dest_rdy.handle, dest_rdy.at(g, 0))
                        pass_gate(pool)
                        scatter(g, u)

            pipeline(pool, turn)
            scatter(NG + 1, 0)
            pool.wait_ge(phase_a_done.handle, 1)
            for p in POOL_PIECES:
                pool.wait_ge(hi_rdy.handle, p + 1)
                pool.tensor_tensor(piece(p, (w1_lo, w2_lo)), piece(p, (w1, w2)), piece(p, (w1_hi, w2_hi)), ALU.subtract
                                   ).then_inc(lo_rdy_pool.handle, 1)
            pool.wait_ge(table_rdy.handle, 1)
            pool.wait_ge(stored.handle, stored.at(NG, 0))

            def add_tile(i, k):
                j = i * RING + k
                pool.wait_ge(y_ev.handle, y_ev.at(j, 1))
                pass_gate(pool)
                for a in range(T):
                    pool.indirect_dma_start(out, bass.IndirectOffsetOnAxis(ap=xt[:, k, a, ID:ID + 1].bitcast(U32), axis=0),
                                            y[:, k % 2, a, :], None, compute_op=ALU.add).then_inc(added.handle, 16)
                pool.wait_ge(added.handle, added.at(j, T))
                pool.sem_inc(tile_done.handle, 1)

            with pool.Fori(0, TILES // RING) as i:
                for k in range(RING):
                    add_tile(i, k)
            for k in range(TILES % RING):
                add_tile(TILES // RING, k)
            pool.wait_ge(stored.handle, stored.at(NG, 0))

        @block.scalar
        def _(act):
            ffn_loads = [
                (w1[:, 0:E // 2], W1[0:E // 2].rearrange("e (c p) n -> p e c n", p=P)),
                (w2[:, 0:E // 2], W2[0:E // 2].rearrange("e (c p) n -> p e c n", p=P)),
                (w1[:, E // 2:], W1[E // 2:].rearrange("e (c p) n -> p e c n", p=P)),
                (w2[:, E // 2:], W2[E // 2:].rearrange("e (c p) n -> p e c n", p=P)),
                (b1c[:], b1.rearrange("e (c p) -> p e c", p=P)),
                (b2_row[:].rearrange("p e n -> p (e n)"), b2.rearrange("(a e) n -> a (e n)", a=1).to_broadcast([P, E * D])),
            ]
            assert len(ffn_loads) == N_FFN
            act.wait_ge(w_ld.handle, 16 * N_W)
            act.activation(gate_tanh[:], gate_in[:], ACT.Tanh).then_inc(tanh_rdy.handle, 1)
            act.activation(bq4[:], bqk[:, 0, :], ACT.Copy, scale=0.25).then_inc(act_step.handle, 1)
            act.wait_ge(act_step.handle, 1)
            give_credit(act, vbd_rdy, p_rdy, h_act, pta)

            def exps(g, n, heads):
                for h in heads:
                    ins = act.activation(s[:, n % 2, h], s[:, n % 2, h], ACT.Exp, bias=nmax[:, n % 2, h:h + 1],
                                         accum_out=z[:, n % 2, h:h + 1])
                if h == HC - 1:
                    ins.then_inc(p_rdy.handle, 1)

            def second_half(g, u):
                act.wait_ge(pt_rdy.handle, pt_rdy.at(g, 2 * u + 2))
                act.wait_ge(pv_rdy.handle, pv_rdy.at(g, u - 1))
                act.activation(pT[:, u % 2, 1], psP[:, 1], ACT.Copy).then_inc(pta.handle, 1)

            def spread_out(g, m):
                act.wait_ge(r_rdy.handle, r_rdy.at(g, m + 1))
                act.wait_ge(a_rdy.handle, a_rdy.at(g, m))
                act.activation(rzT[:].rearrange("p c k -> p (c k)"), psA[:, 2:4].rearrange("p c k -> p (c k)"),
                               ACT.Copy).then_inc(r_ev.handle, 1)

            def values_apart(g, n):
                b, c = n % UNITS // KC, n % KC
                if n == UNITS:
                    act.wait_ge(v_rdy.handle, v_rdy.at(g, 3))
                if n == 2 * KC:
                    act.wait_ge(v_rdy.handle, v_rdy.at(g, 2))
                act.wait_ge(pv_rdy.handle, pv_rdy.at(g, n - 3))
                dst = vbd[:, b % 2, c * HC:(c + 1) * HC, :].rearrange("p h k -> p (h k)")
                act.activation(strided(dst, HC, P + DH, DH), v[:, b, c * P:(c + 1) * P].rearrange("p (h d) -> p h d", h=HC), ACT.Copy
                               ).then_inc(vbd_rdy.handle, 1)

            def ctx_out(g, c):
                act.wait_ge(cT_rdy.handle, cT_rdy.at(g, KC + c + 1))
                act.activation(cT[:, c], psW[:], ACT.Copy).then_inc(cT_ev.handle, 1)

            def xT_out(g, c):
                act.wait_ge(xT_rdy.handle, xT_rdy.at(g, KC + c + 1))
                act.activation(xT[:, c], psW[:], ACT.Copy).then_inc(xT_ev.handle, 1)

            def x2T_out(g, c):
                act.wait_ge(t2_rdy.handle, t2_rdy.at(g, c + 1 - KC))
                act.activation(x2T[:, c], psW[:], ACT.Copy).then_inc(t2_ev.handle, 1)

            def q_out(g, c):
                act.wait_ge(q_rdy.handle, q_rdy.at(g, KC + c + 1))
                act.wait_ge(s_rdy.handle, s_rdy.at(g, UNITS - 1 + c))
                act.wait_ge(q_split.handle, q_split.at(g, KC + c))
                act.activation(q_f[:], psW[:], ACT.Identity, bias=bq4[:, c:c + 1], scale=0.25).then_inc(q_ev.handle, 1)
                act.wait_ge(q_ev.handle, q_ev.at(g, KC + c + 1))
                act.activation(q_hi[:, c], q_f[:], ACT.Copy).then_inc(q_hi_rdy.handle, 1)

            def k_out(g, c):
                act.wait_ge(k_rdy.handle, k_rdy.at(g, KC + c + 1))
                act.wait_ge(kbd_rdy.handle, kbd_rdy.at(g, UNITS - 1 + c))
                act.wait_ge(k_split.handle, k_split.at(g, KC + c))
                act.activation(k_f[:], psW[:], ACT.Identity, bias=bqk[:, 1, c:c + 1]).then_inc(k_ev.handle, 1)
                act.wait_ge(k_ev.handle, k_ev.at(g, KC + c + 1))
                act.activation(k_hi[:, c], k_f[:], ACT.Copy).then_inc(k_hi_rdy.handle, 1)

            def turn(g, has_tail, has_attention, has_next):
                for u in range(UNITS):
                    n = u + 1
                    has_exp = has_attention if n < UNITS else has_next
                    if u % 2 == 0 and (has_attention if u else has_tail):
                        spread_out(g, u // 2 - 1)
                    if isinstance(g, int) and g == -1 and u == 1:
                        act.wait_ge(c_ld.handle, c_ld.at(0, 1))
                        act.wait_ge(x_ld.handle, x_ld.at(0, 1))
                        with nc.allow_non_contiguous_dma(reason="bias columns, once"):
                            for dst, src in ffn_loads:
                                act.dma_start(dst, src).then_inc(ffn_ld.handle, 16)
                    if has_exp:
                        act.wait_ge(mx_rdy.handle, mx_rdy.at(g, n + 1))
                        act.wait_ge(rz_rdy.handle, rz_rdy.at(g, n - 1))
                        exps(g, n, range(0, 2))
                    if has_attention:
                        second_half(g, u)
                    if has_next and u == 0:
                        ctx_out(g, 0)
                    if has_tail and u == 3:
                        x2T_out(g, 1)
                    if has_next and u == 4:
                        xT_out(g, 1)
                    if has_next and u >= 5 and u <= 6:
                        q_out(g, u - 5)
                    if has_tail and u == 4:
                        act.wait_ge(lm_rdy.handle, lm_rdy.at(g, 0))
                        act.activation(prob[:], logit[:], ACT.Exp, scale=1.0 / TEMP).then_inc(ex_rdy.handle, 1)
                    if has_exp:
                        exps(g, n, range(2, 6))
                    if has_next and u == 0:
                        ctx_out(g, 1)
                    if has_tail and u == 2:
                        x2T_out(g, 0)
                    if has_next and u == 3:
                        xT_out(g, 0)
                    if has_next and u >= 4 and u <= 5:
                        k_out(g, u - 4)
                    if has_exp:
                        exps(g, n, range(6, HC))
                    if has_attention if u + 3 < UNITS else has_next:
                        values_apart(g, u + 3)

            pipeline(act, turn)
            act.wait_ge(phase_a_done.handle, 1)
            for p in range(2 * E):
                act.activation(piece(p, (w1_hi, w2_hi)), piece(p, (w1, w2)), ACT.Copy).then_inc(hi_rdy.handle, 1)

            def first_weights_hi(j, s):
                e = act.value_load(tile_exp[0:1, bass.ds(j, 1)], min_val=0, max_val=E - 1)
                act.wait_ge(h_rdy.handle, h_rdy.at(j, -2))
                act.activation(w1s_hi[:, s].rearrange("p c n -> p (c n)"), w1_hi[:, bass.ds(e, 1)].rearrange("p e c n -> p (e c n)"),
                               ACT.Copy).then_inc(hi_copied.handle, 1)

            def gelu_tile(i, k):
                j = i * RING + k
                for q in range(2):
                    act.wait_ge(h_rdy.handle, h_rdy.at(j, q + 1))
                    if q == 0:
                        act.wait_ge(y_rdy.handle, y_rdy.at(j, -1))
                    if q == 0:
                        act.wait_ge(lo_copied.handle, lo_copied.at(j, 1))
                    act.wait_ge(h_split.handle, h_split.at(j, q - 1))
                    for m in range(2 * q, 2 * q + 2):
                        h = bank[2 * (k % 2) + q][:, (m % 2) * TR:(m % 2 + 1) * TR]
                        act.activation(hT[:, m], h, ACT.Gelu, bias=b1s[:, k % 2, m:m + 1])
                        ins = act.activation(h_hi[:, k % 2, m], h, ACT.Gelu, bias=b1s[:, k % 2, m:m + 1])
                    ins.then_inc(h_act.handle, 1)

            act.wait_ge(table_rdy.handle, 1)
            act.wait_ge(hi_rdy.handle, 2 * E)
            act.activation(gelu_loaded[:], gate_in[:, 0:1], ACT.Gelu)
            first_weights_hi(0, 0)
            first_weights_hi(1, 1)
            with act.Fori(0, TILES // RING) as i:
                for k in range(RING):
                    gelu_tile(i, k)
                    first_weights_hi(i * RING + k + 2, k % 2)
            for k in range(TILES % RING):
                gelu_tile(TILES // RING, k)
                if k + 2 < TILES % RING:
                    first_weights_hi(TILES - TILES % RING + k + 2, k % 2)

        @block.vector
        def _(dve):
            give_credit(dve, v_rdy, kbd_dve, q_split, k_split, h_split, xn_rdy, sm_rdy, rz_rdy, ptd, a_rdy, x1_rdy, xn2_rdy, xe_ev, y_ev)
            dve_step = signal("dve_step")
            DVE_STEPS = 28
            steps = [0]

            def link(ins, g, alone=False):
                steps[0] += 1
                ins.then_inc(dve_step.handle, 1)
                dve.wait_ge(dve_step.handle, (g - 1) * DVE_STEPS + steps[0])
                if alone:
                    pass_gate(dve)

            def mark(ins):
                steps[0] += 1
                ins.then_inc(dve_step.handle, 1)

            dve.wait_ge(w_ld.handle, 16 * N_W)
            dve.wait_ge(tanh_rdy.handle, 1)
            dve.wait_ge(const.handle, 9)
            dve.wait_ge(setup.handle, 10)
            dve.tensor_copy(base[:], erow[:])

            def statistics(g):
                dve.wait_ge(x_ld.handle, x_ld.at(g, 2))
                for b in range(G):
                    ins = dve.bn_stats(stat[:, b], xg[:, b])
                ins.then_inc(stat_rdy.handle, 1)
                dve.wait_ge(stat_rdy.handle, stat_rdy.at(g, 2))
                pass_gate(dve)
                for b in range(G):
                    ins = dve.bn_aggr(mv[:, b], stat[:, b])
                ins.then_inc(mv_rdy.handle, 1)

            def normal_x(g):
                dve.wait_ge(mv_rdy.handle, mv_rdy.at(g, 2))
                dve.wait_ge(rstd_rdy.handle, rstd_rdy.at(g, 2))
                dve.wait_ge(xT_rdy.handle, xT_rdy.at(g, KC))
                for b in range(G):
                    ins = dve.tensor_scalar(xn[:, b], xg[:, b], mv[:, b, 0:1], rstd[:, b:b + 1], ALU.subtract, ALU.mult)
                ins.then_inc(xn_rdy.handle, 1)

            def values_out(g, j):
                dve.wait_ge(v_ps.handle, v_ps.at(g, 2 + j + 1))
                dve.wait_ge(vbd_rdy.handle, vbd_rdy.at(g, 4 * j + 4))
                dve.tensor_tensor(v[:, 2 * j:2 * j + 2], psW[:].rearrange("p (b n) -> p b n", b=2),
                                  bv_row[:].unsqueeze(1).to_broadcast([P, 2, D]), ALU.add).then_inc(v_rdy.handle, 1)

            def q_low(g, c):
                dve.wait_ge(q_hi_rdy.handle, q_hi_rdy.at(g, KC + c + 1))
                dve.wait_ge(s_rdy.handle, s_rdy.at(g, UNITS - 1 + c))
                dve.tensor_tensor(q_lo[:, c], q_f[:], q_hi[:, c], ALU.subtract).then_inc(q_split.handle, 1)

            def k_low(g, c):
                dve.wait_ge(k_hi_rdy.handle, k_hi_rdy.at(g, KC + c + 1))
                dve.wait_ge(kbd_rdy.handle, kbd_rdy.at(g, UNITS - 1 + c))
                dve.wait_ge(kbd_dve.handle, kbd_dve.at(g, DVE_UNITS))
                dve.tensor_tensor(k_lo[:, c], k_f[:], k_hi[:, c], ALU.subtract).then_inc(k_split.handle, 1)

            def keys_lo_apart(g, n):
                b, c = n % UNITS // KC, n % KC
                dve.wait_ge(k_split.handle, k_split.at(g, (n // UNITS) * KC + (c + 1 if n < UNITS + KC else KC)))
                dve.wait_ge(s_rdy.handle, s_rdy.at(g, n - 1))
                dve.tensor_tensor(kbd[1][:, n % 2], k_lo[:, c, b * P:(b + 1) * P].unsqueeze(1).to_broadcast([P, HC, P]),
                                  head_mask[:].unsqueeze(2).to_broadcast([P, HC, P]), ALU.mult).then_inc(kbd_dve.handle, 1)

            def row_max(g, n):
                b = n % UNITS // KC
                if n == 2 * KC:
                    dve.wait_ge(m_ld[1].handle, m_ld[1].at(g, 1))
                if n == UNITS:
                    dve.wait_ge(m_ld[0].handle, m_ld[0].at(g, 2))
                dve.wait_ge(pt_rdy.handle, pt_rdy.at(g, 2 * n - 2))
                for j in range(2):
                    dve.wait_ge((s_half, s_rdy)[j].handle, (s_half, s_rdy)[j].at(g, n + 1))
                    ins = dve.tensor_tensor(s[:, n % 2, 4 * j:4 * j + 4], psS[:, n % 2, 4 * j:4 * j + 4],
                                            mg[:, b].unsqueeze(1).to_broadcast([P, HC // 2, P]), ALU.add)
                ins.then_inc(sm_rdy.handle, 1)
                dve.wait_ge(sm_rdy.handle, sm_rdy.at(g, n + 1))
                dve.wait_ge(p_rdy.handle, p_rdy.at(g, n - 1))
                dve.tensor_reduce(nmax[:, n % 2], s[:, n % 2], AX_X, ALU.max, negate=True).then_inc(mx_rdy.handle, 1)

            def residual(g, b):
                dve.wait_ge(proj_rdy.handle, proj_rdy.at(g, b + 1))
                if b == 0:
                    dve.wait_ge(xb_rdy.handle, xb_rdy.at(g, 1))
                    dve.wait_ge(stored.handle, stored.at(g, 0))
                    dve.wait_ge(xn2_rdy.handle, xn2_rdy.at(g, 0))
                dve.scalar_tensor_tensor(x1[:, b % G], psW[:, 0:D], gate_tanh[:, 0:1], xb[:, b % G], ALU.mult, ALU.add
                                         ).then_inc(x1_rdy.handle, 1)

            def first_half(g, u):
                dve.wait_ge(p_rdy.handle, p_rdy.at(g, u + 1))
                dve.reciprocal(rz8[:, u % 2], z[:, u % 2]).then_inc(rz_rdy.handle, 1)
                dve.wait_ge(pt_rdy.handle, pt_rdy.at(g, 2 * u + 1))
                dve.wait_ge(pv_rdy.handle, pv_rdy.at(g, u - 1))
                dve.tensor_copy(pT[:, u % 2, 0], psP[:, 0]).then_inc(ptd.handle, 1)
                dve.wait_ge(rz_rdy.handle, rz_rdy.at(g, u + 1))
                dve.wait_ge(r_rdy.handle, r_rdy.at(g, u // 2))
                dve.tensor_copy(rz[:, u % 2], rz8[:, u % 2].unsqueeze(2).to_broadcast([P, HC, DH])).then_inc(rz_spread.handle, 1)

            def normalize(g, m):
                dve.wait_ge(pv_rdy.handle, pv_rdy.at(g, 2 * m + 2))
                dve.wait_ge(r_ev.handle, r_ev.at(g, m + 1))
                dve.wait_ge(proj_rdy.handle, proj_rdy.at(g, m))
                dve.tensor_tensor(aT[:], psA[:, 0:2], rzT[:], ALU.mult).then_inc(a_rdy.handle, 1)

            def statistics2(g):
                dve.wait_ge(x1_rdy.handle, x1_rdy.at(g, 0))
                for b in range(G):
                    ins = dve.bn_stats(stat2[:, b], x1[:, b])
                ins.then_inc(stat2_rdy.handle, 1)
                dve.wait_ge(stat2_rdy.handle, stat2_rdy.at(g, 0))
                pass_gate(dve)
                for b in range(G):
                    ins = dve.bn_aggr(mv2[:, b], stat2[:, b])
                ins.then_inc(mv2_rdy.handle, 1)

            def normal_x1(g):
                dve.wait_ge(mv2_rdy.handle, mv2_rdy.at(g, 0))
                dve.wait_ge(rstd2_rdy.handle, rstd2_rdy.at(g, 0))
                for b in range(G):
                    ins = dve.tensor_scalar(xn2[:, b], x1[:, b], mv2[:, b, 0:1], rstd2[:, b:b + 1], ALU.subtract, ALU.mult)
                ins.then_inc(xn2_rdy.handle, 1)
                link(dve.tensor_copy(rows[:, :, ID].bitcast(U32), token[:]), g)
                mark(dve.tensor_scalar(token[:], token[:], float(G * P), None, ALU.add))

            def logits_out(g):
                dve.wait_ge(lg_rdy.handle, lg_rdy.at(g, 0))
                dve.tensor_tensor(logit[:], psW[:, 0:G * E].rearrange("p (g e) -> p g e", g=G),
                                  bg_row[:].unsqueeze(1).to_broadcast([P, G, E]), ALU.add).then_inc(lg_ev.handle, 1)

            def logits_less_max(g):
                dve.wait_ge(lg_ev.handle, lg_ev.at(g, 0))
                link(dve.tensor_reduce(nlmax[:], logit[:], AX_X, ALU.max), g)
                dve.tensor_tensor(logit[:], logit[:], nlmax[:].unsqueeze(2).to_broadcast([P, G, E]), ALU.subtract
                                  ).then_inc(lm_rdy.handle, 1)

            def two_best(g):
                dve.wait_ge(ex_rdy.handle, ex_rdy.at(g, 0))
                pass_gate(dve)
                for b in range(G):
                    mark(dve.max(top[:, b], prob[:, b]))
                dve.wait_ge(dve_step.handle, (g - 1) * DVE_STEPS + steps[0])
                pass_gate(dve)
                for b in range(G - 1):
                    mark(dve.max_index(topi[:, b], top[:, b], prob[:, b]))
                link(dve.max_index(topi[:, G - 1], top[:, G - 1], prob[:, G - 1]), g)
                link(dve.tensor_copy(topf[:], topi[:, :, 0:2]), g)
                mark(dve.tensor_tensor(gsum[:], top[:, :, 0], top[:, :, 1], ALU.add))
                mark(dve.tensor_tensor(one1[:], expert_no[:].unsqueeze(1).to_broadcast([P, G, E]),
                                       topf[:, :, 0:1].to_broadcast([P, G, E]), ALU.is_equal))
                link(dve.tensor_tensor(one2[:], expert_no[:].unsqueeze(1).to_broadcast([P, G, E]),
                                       topf[:, :, 1:2].to_broadcast([P, G, E]), ALU.is_equal), g)
                dve.tensor_tensor(pick16[:], one1[:], one2[:], ALU.add).then_inc(pick_rdy.handle, 1)
                mark(dve.tensor_tensor(slot[:], one1[:], top[:, :, 0:1].to_broadcast([P, G, E]), ALU.mult))
                mark(dve.tensor_tensor(pick[:], one2[:], top[:, :, 1:2].to_broadcast([P, G, E]), ALU.mult))
                link(dve.tensor_reduce(nlmax[:], prob[:], AX_X, ALU.add), g)
                mark(dve.tensor_tensor(gate, slot[:], pick[:], ALU.add))
                link(dve.scalar_tensor_tensor(gsum[:], nlmax[:], GATE_EPS, gsum[:], ALU.mult, ALU.add), g)
                link(dve.reciprocal(nlmax[:], gsum[:]), g)
                link(dve.tensor_scalar(nlmax[:], nlmax[:], gate_tanh[:, 1:2], None, ALU.mult), g)
                mark(dve.tensor_tensor(gate, gate, nlmax[:].unsqueeze(2).to_broadcast([P, G, E]), ALU.mult))

            def ranks_out(g):
                dve.wait_ge(rank_rdy.handle, rank_rdy.at(g, 0))
                mark(dve.tensor_tensor(slot[:], psW[:, 0:G * E].rearrange("p (g e) -> p g e", g=G),
                                       base[:].unsqueeze(1).to_broadcast([P, G, E]), ALU.add))
                dve.wait_ge(dve_step.handle, (g - 1) * DVE_STEPS + steps[0])
                dve.tensor_tensor(base[:], base[:], psW[:, G * E:(G + 1) * E], ALU.add).then_inc(rank_ev.handle, 1)

            def destinations(g):
                mark(dve.tensor_tensor(one1[:], one1[:], slot[:], ALU.mult))
                link(dve.tensor_tensor(one2[:], one2[:], slot[:], ALU.mult), g)
                mark(dve.tensor_reduce(dest[:, 0], one1[:], AX_X, ALU.add))
                link(dve.tensor_reduce(dest[:, 1], one2[:], AX_X, ALU.add), g)
                dve.tensor_copy(dest_no[:], dest[:]).then_inc(dest_rdy.handle, 1)
                assert steps[0] == DVE_STEPS, steps

            def turn(g, has_tail, has_attention, has_next):
                steps[0] = 0
                for u in range(UNITS):
                    if u % 2 == 0 and (has_attention if u else has_tail):
                        normalize(g, u // 2 - 1)
                    if has_next and not has_attention and u == 0:
                        statistics(g)
                    if has_attention:
                        first_half(g, u)
                    if (u + 3) % UNITS < DVE_UNITS and (has_attention if u + 3 < UNITS else has_next):
                        keys_lo_apart(g, u + 3)
                    if has_next and u == 6:
                        q_low(g, 1)
                    if has_next and u == 1:
                        values_out(g, 0)
                    if has_next and u == 3:
                        normal_x(g)
                    if has_tail and u == 3:
                        logits_out(g)
                    if has_tail and u == 5:
                        ranks_out(g)
                    if u < 6 and u % 2 == 0 and (has_attention if u else has_tail):
                        residual(g, u // 2 - 1)
                    if has_next and u == 7:
                        values_out(g, 1)
                    if has_attention if u + 2 < UNITS else has_next:
                        row_max(g, u + 2)
                    if has_next and u == 5:
                        q_low(g, 0)
                    if has_attention and u == 6:
                        residual(g, 2)
                    if has_tail and u == 0:
                        statistics2(g)
                    if has_tail and u == 1:
                        normal_x1(g)
                    if has_next and has_attention and u == 2:
                        statistics(g)
                    if has_tail and u == 3:
                        logits_less_max(g)
                    if has_tail and u == 4:
                        two_best(g)
                    if has_tail and u == 5:
                        destinations(g)
                    if has_next and u >= 4 and u <= 5:
                        k_low(g, u - 4)

            pipeline(dve, turn)
            steps[0] = 0
            dve.wait_ge(rank_ev.handle, rank_ev.at(NG, 0))
            dve.wait_ge(dest_rdy.handle, dest_rdy.at(NG, 0))
            dve.wait_ge(stored.handle, stored.at(NG, 0))
            dve.wait_ge(ffn_ld.handle, 16 * N_FFN)
            dve.sem_inc(phase_a_done.handle, 1)

            def chain(ins):
                steps[0] += 1
                ins.then_inc(dve_step.handle, 1)
                dve.wait_ge(dve_step.handle, NG * DVE_STEPS + steps[0])

            chain(dve.tensor_tensor(ends[:], base[0:1], erow[0:1], ALU.subtract))
            chain(dve.tensor_tensor(over[:], ends[:].unsqueeze(2).to_broadcast([1, E, MAXT]),
                                    tile_edge[:].unsqueeze(1).to_broadcast([1, E, MAXT]), ALU.is_gt))
            chain(dve.tensor_reduce(n_tiles[:], over[:], AX_X, ALU.add))
            chain(dve.tensor_copy(ends[:], n_tiles[:]))
            for e in range(1, E):
                chain(dve.tensor_tensor(ends[:, e:e + 1], ends[:, e:e + 1], ends[:, e - 1:e], ALU.add))
            chain(dve.tensor_tensor(past[:], tile_no[:].unsqueeze(2).to_broadcast([1, LISTED, E]),
                                    ends[:].unsqueeze(1).to_broadcast([1, LISTED, E]), ALU.is_ge))
            chain(dve.tensor_tensor(past_n[:], past[:], n_tiles[:].unsqueeze(1).to_broadcast([1, LISTED, E]), ALU.mult))
            chain(dve.tensor_reduce(t_exp[:], past[:], AX_X, ALU.add))
            chain(dve.tensor_reduce(t_row[:], past_n[:], AX_X, ALU.add))
            chain(dve.tensor_tensor(t_row[:], tile_no[:], t_row[:], ALU.subtract))
            chain(dve.tensor_scalar(t_row[:], t_row[:], float(TR), None, ALU.mult))
            chain(dve.scalar_tensor_tensor(t_row[:], t_exp[:], float(CAP), t_row[:], ALU.mult, ALU.add))
            chain(dve.tensor_scalar(t_row[:], t_row[:], float(DUMMY), None, ALU.min))
            chain(dve.tensor_scalar(t_exp[:], t_exp[:], float(E - 1), None, ALU.min))
            chain(dve.tensor_copy(tile_row[:], t_row[:]))
            chain(dve.tensor_copy(tile_exp[:], t_exp[:]))
            dve.tensor_copy(pad_row[:], base[0:1]).then_inc(table_rdy.handle, 1)

            for p in DVE_PIECES:
                dve.wait_ge(hi_rdy.handle, p + 1)
                dve.tensor_tensor(piece(p, (w1_lo, w2_lo)), piece(p, (w1, w2)), piece(p, (w1_hi, w2_hi)), ALU.subtract
                                  ).then_inc(lo_rdy.handle, 1)

            def x_out(i, k):
                j = i * RING + k
                dve.wait_ge(xe_rdy.handle, xe_rdy.at(j, 1))
                hi = xe_hi[:, k % 2].rearrange("p c n -> p (c n)")
                dve.tensor_copy(hi, psW[:]).then_inc(xh_rdy.handle, 1)
                dve.wait_ge(xh_rdy.handle, xh_rdy.at(j, 1))
                dve.tensor_tensor(xe_lo[:, k % 2].rearrange("p c n -> p (c n)"), psW[:], hi, ALU.subtract).then_inc(xe_ev.handle, 1)

            def first_weights(j, s):
                e = dve.value_load(tile_exp[0:1, bass.ds(j, 1)], min_val=0, max_val=E - 1)
                dve.wait_ge(h_act.handle, h_act.at(j, -2))
                dve.tensor_copy(b1s[:, s], b1c[:, bass.ds(e, 1), :].rearrange("p e m -> p (e m)"))
                dve.tensor_copy(w1s_lo[:, s].rearrange("p c n -> p (c n)"), w1_lo[:, bass.ds(e, 1)].rearrange("p e c n -> p (e c n)")
                                ).then_inc(lo_copied.handle, 1)

            def h_out(i, k, q):
                j = i * RING + k
                dve.wait_ge(h_act.handle, h_act.at(j, q + 1))
                dve.tensor_tensor(h_lo[:, k % 2, 2 * q:2 * q + 2], hT[:, 2 * q:2 * q + 2], h_hi[:, k % 2, 2 * q:2 * q + 2],
                                  ALU.subtract).then_inc(h_split.handle, 1)

            def y_out(i, k):
                j = i * RING + k
                e = dve.value_load(tile_exp[0:1, bass.ds(j, 1)], min_val=0, max_val=E - 1)
                dve.wait_ge(y_rdy.handle, y_rdy.at(j, 1))
                dve.wait_ge(tile_done.handle, tile_done.at(j, -1))
                dve.tensor_tensor(y[:, k % 2], psP[:, k % 2].rearrange("p (a n) -> p a n", a=T),
                                  b2_row[:, bass.ds(e, 1)].to_broadcast([P, T, D]), ALU.add).then_inc(y_step.handle, 1)
                dve.wait_ge(y_step.handle, y_step.at(j, 1))
                for a in range(T):
                    ins = dve.tensor_scalar(y[:, k % 2, a], y[:, k % 2, a], xt[:, k, a, bass.ds(e + D, 1)], None, ALU.mult)
                ins.then_inc(y_ev.handle, 1)

            dve.wait_ge(lo_rdy.handle, len(DVE_PIECES))
            dve.wait_ge(lo_rdy_pool.handle, len(POOL_PIECES))
            first_weights(0, 0)
            x_out(0, 0)
            first_weights(1, 1)
            h_out(0, 0, 0)
            x_out(0, 1)
            h_out(0, 0, 1)
            with dve.Fori(0, TILES // RING) as i:
                for k in range(RING):
                    first_weights(i * RING + k + 2, k % 2)
                    h_out(i + (k + 1) // RING, (k + 1) % RING, 0)
                    x_out(i + (k + 2) // RING, (k + 2) % RING)
                    h_out(i + (k + 1) // RING, (k + 1) % RING, 1)
                    y_out(i, k)
            for k in range(TILES % RING):
                if k + 2 < TILES % RING:
                    first_weights(TILES - TILES % RING + k + 2, k % 2)
                if k + 1 < TILES % RING:
                    h_out(TILES // RING, k + 1, 0)
                if k + 2 < TILES % RING:
                    x_out(TILES // RING, k + 2)
                if k + 1 < TILES % RING:
                    h_out(TILES // RING, k + 1, 1)
                y_out(TILES // RING, k)

        @block.tensor
        def _(pe):
            give_credit(pe, h_rdy, cT_rdy, xT_rdy, s_rdy, pt_rdy, pv_rdy, r_rdy, proj_rdy, y_rdy)
            pe.wait_ge(w_ld.handle, 16 * N_W)
            pe.wait_ge(const.handle, 8)

            def scores(g, n, j):
                b, c = n % UNITS // KC, n % KC
                if j == 0:
                    if n >= UNITS:
                        pe.wait_ge(q_split.handle, q_split.at(g, KC + c + 1))
                    pe.wait_ge(sm_rdy.handle, sm_rdy.at(g, n - 1))
                    pe.wait_ge(kbd_rdy.handle, kbd_rdy.at(g, n + 1))
                    if n % UNITS < DVE_UNITS:
                        pe.wait_ge(kbd_dve.handle, kbd_dve.at(g, n // UNITS * DVE_UNITS + n % UNITS + 1))
                for m, (q, ks) in enumerate(((q_hi, kbd[0]), (q_hi, kbd[1]), (q_lo, kbd[0]))):
                    ins = pe.matmul(psS[:, n % 2, 4 * j:4 * j + 4], q[:, c, b * P:(b + 1) * P], ks[:, n % 2, 4 * j:4 * j + 4],
                                    start=(m == 0), stop=(m == 2))
                ins.then_inc((s_half, s_rdy)[j].handle, 1)

            def probs_transposed(g, u):
                pe.wait_ge(p_rdy.handle, p_rdy.at(g, u + 1))
                for j in range(2):
                    pe.wait_ge((ptd, pta)[j].handle, (ptd, pta)[j].at(g, u))
                    for h in range(4):
                        ins = pe.transpose(psP[:, j, h * P:(h + 1) * P], s[:, u % 2, 4 * j + h], ident[:])
                    ins.then_inc(pt_rdy.handle, 1)

            def attention_out(g, u):
                b, c = u // KC, u % KC
                pe.wait_ge(vbd_rdy.handle, vbd_rdy.at(g, u + 1))
                if c == 0:
                    pe.wait_ge(a_rdy.handle, a_rdy.at(g, b))
                for j in range(2):
                    pe.wait_ge((ptd, pta)[j].handle, (ptd, pta)[j].at(g, u + 1))
                    for h in range(4):
                        hh = 4 * j + h
                        ins = pe.matmul(psA[:, c], vbd[:, b % 2, c * HC + hh], pT[:, u % 2, j, h * P:(h + 1) * P],
                                        start=(hh == 0), stop=(hh == HC - 1))
                ins.then_inc(pv_rdy.handle, 1)
                if c == 1:
                    pe.wait_ge(rz_spread.handle, rz_spread.at(g, u + 1))
                    for k in range(KC):
                        ins = pe.transpose(psA[:, 2 + k], rz[:, k].rearrange("p h d -> p (h d)"), ident[:])
                    ins.then_inc(r_rdy.handle, 1)

            def ctx_transposed(g, c):
                if c == 0:
                    pe.wait_ge(v_rdy.handle, v_rdy.at(g, 2))
                    pe.wait_ge(c_ld.handle, c_ld.at(g, 2))
                else:
                    pe.wait_ge(cT_ev.handle, cT_ev.at(g, KC + 1))
                    pe.wait_ge(x1_rdy.handle, x1_rdy.at(g, 0))
                for b in range(G):
                    ins = pe.transpose(psW[:, b * P:(b + 1) * P], cg[:, b, c * P:(c + 1) * P], ident[:])
                ins.then_inc(cT_rdy.handle, 1)

            def x_transposed(g, c, has_tail, has_attention):
                if c == 0:
                    pe.wait_ge(xn_rdy.handle, xn_rdy.at(g, 2))
                    pe.wait_ge(v_rdy.handle, v_rdy.at(g, 3))
                    if has_attention:
                        pe.wait_ge(x1_rdy.handle, x1_rdy.at(g, 1))
                    if has_tail:
                        pe.wait_ge(lg_ev.handle, lg_ev.at(g, 0))
                else:
                    pe.wait_ge(xT_ev.handle, xT_ev.at(g, KC + 1))
                for b in range(G):
                    ins = pe.transpose(psW[:, b * P:(b + 1) * P], xn[:, b, c * P:(c + 1) * P], ident[:])
                ins.then_inc(xT_rdy.handle, 1)

            def queries(g, c):
                pe.wait_ge(k_ev.handle, k_ev.at(g, KC + c + 1))
                for k in range(KC):
                    ins = pe.matmul(psW[:], wq[:, k, c * P:(c + 1) * P], xT[:, k], start=(k == 0), stop=(k == KC - 1))
                ins.then_inc(q_rdy.handle, 1)

            def keys(g, c, has_tail, has_attention):
                if c == 0:
                    pe.wait_ge(xT_ev.handle, xT_ev.at(g, 2 * KC))
                    if has_attention:
                        pe.wait_ge(x1_rdy.handle, x1_rdy.at(g, 2))
                else:
                    pe.wait_ge(q_ev.handle, q_ev.at(g, KC + 1))
                    if has_tail:
                        pe.wait_ge(rank_ev.handle, rank_ev.at(g, 0))
                for k in range(KC):
                    ins = pe.matmul(psW[:], wkv[:, k, c * P:(c + 1) * P], cT[:, k], start=(k == 0), stop=(k == KC - 1))
                ins.then_inc(k_rdy.handle, 1)

            def values(g, j, has_attention):
                if j == 0:
                    pe.wait_ge(cT_ev.handle, cT_ev.at(g, 2 * KC))
                else:
                    pe.wait_ge(q_ev.handle, q_ev.at(g, 2 * KC))
                    if has_attention:
                        pe.wait_ge(x1_rdy.handle, x1_rdy.at(g, 3))
                for b in range(2 * j, 2 * j + 2):
                    o = psW[:, (b % 2) * D:(b % 2 + 1) * D]
                    for k in range(KC):
                        ins = pe.matmul(o, cT[:, k, b * P:(b + 1) * P], wkv[:, k, D:2 * D], start=(k == 0), stop=(k == KC - 1))
                ins.then_inc(v_ps.handle, 1)

            def project(g, b, has_tail, has_attention, has_next):
                pe.wait_ge(a_rdy.handle, a_rdy.at(g, b + 1))
                pe.wait_ge(x1_rdy.handle, x1_rdy.at(g, b))
                if b == -1 and has_attention:
                    pe.wait_ge(v_rdy.handle, v_rdy.at(g, 2))
                if b == -1 and has_next:
                    pe.wait_ge(cT_ev.handle, cT_ev.at(g, KC + 1))
                if b == 0 and has_next:
                    pe.wait_ge(v_rdy.handle, v_rdy.at(g, 3))
                if b == 1 and has_tail:
                    pe.wait_ge(lg_ev.handle, lg_ev.at(g, 0))
                if b == 1 and has_next:
                    pe.wait_ge(xT_ev.handle, xT_ev.at(g, 2 * KC))
                if b == 2 and has_tail:
                    pe.wait_ge(rank_ev.handle, rank_ev.at(g, 0))
                if b == 2 and has_next:
                    pe.wait_ge(q_ev.handle, q_ev.at(g, 2 * KC))
                for k in range(KC):
                    ins = pe.matmul(psW[:, 0:D], aT[:, k], wp[:, k], start=(k == 0), stop=(k == KC - 1))
                ins.then_inc(proj_rdy.handle, 1)

            def x1_transposed(g, c, has_attention):
                if c == 0:
                    pe.wait_ge(xn2_rdy.handle, xn2_rdy.at(g, 0))
                    if has_attention:
                        pe.wait_ge(x1_rdy.handle, x1_rdy.at(g, 1))
                else:
                    pe.wait_ge(t2_ev.handle, t2_ev.at(g, 1 - KC))
                for b in range(G):
                    ins = pe.transpose(psW[:, b * P:(b + 1) * P], xn2[:, b, c * P:(c + 1) * P], ident[:])
                ins.then_inc(t2_rdy.handle, 1)

            def router(g):
                pe.wait_ge(t2_ev.handle, t2_ev.at(g, 0))
                for b in range(G):
                    for k in range(KC):
                        ins = pe.matmul(psW[:, b * E:(b + 1) * E], x2T[:, k, b * P:(b + 1) * P], wg[:, k], start=(k == 0), stop=(k == KC - 1))
                ins.then_inc(lg_rdy.handle, 1)

            def ranks(g, has_attention, has_next):
                pe.wait_ge(pick_rdy.handle, pick_rdy.at(g, 0))
                if has_attention:
                    pe.wait_ge(x1_rdy.handle, x1_rdy.at(g, 2))
                if has_next:
                    pe.wait_ge(q_ev.handle, q_ev.at(g, KC + 1))
                pe.matmul(psW[:, 0:G * E], before16[:], pick16[:].rearrange("p g e -> p (g e)"), start=True, stop=False, skip_group_check=True)
                for b in range(G - 1):
                    pe.matmul(psW[:, (b + 1) * E:G * E].rearrange("p (g e) -> p g e", e=E), ones16[:],
                              pick16[:, b:b + 1].to_broadcast([P, G - 1 - b, E]), start=False, stop=False, skip_group_check=True)
                for b in range(G):
                    ins = pe.matmul(psW[:, G * E:(G + 1) * E], ones16[:], pick16[:, b], start=False, stop=(b == G - 1), skip_group_check=True)
                ins.then_inc(rank_rdy.handle, 1)

            def turn(g, has_tail, has_attention, has_next):
                for u in range(UNITS):
                    has_scores = has_attention if u + 2 < UNITS else has_next
                    if has_attention:
                        probs_transposed(g, u)
                    if has_next and u == 0:
                        ctx_transposed(g, 0)
                    if has_next and u == 1:
                        values(g, 0, has_attention)
                    if has_tail and u == 3:
                        x1_transposed(g, 1, has_attention)
                    if has_next and u == 4:
                        x_transposed(g, 1, has_tail, has_attention)
                    if has_next and u >= 5 and u <= 6:
                        queries(g, u - 5)
                    if has_scores:
                        scores(g, u + 2, 0)
                    if u < 6 and u % 2 == 0 and (has_attention if u else has_tail):
                        project(g, u // 2 - 1, has_tail, has_attention, has_next)
                    if has_tail and u == 3:
                        router(g)
                    if has_tail and u == 5:
                        ranks(g, has_attention, has_next)
                    if has_next and u == 7:
                        values(g, 1, has_attention)
                    if has_scores:
                        scores(g, u + 2, 1)
                    if has_attention and u == 6:
                        project(g, 2, has_tail, has_attention, has_next)
                    if has_next and u == 0:
                        ctx_transposed(g, 1)
                    if has_tail and u == 2:
                        x1_transposed(g, 0, has_attention)
                    if has_next and u == 3:
                        x_transposed(g, 0, has_tail, has_attention)
                    if has_next and u >= 4 and u <= 5:
                        keys(g, u - 4, has_tail, has_attention)
                    if has_attention:
                        attention_out(g, u)

            pipeline(pe, turn)

            def tile_transposed(i, k):
                j = i * RING + k
                pe.wait_ge(xt_ld[k].handle, xt_ld[k].at(i, 1))
                pe.wait_ge(xe_ev.handle, xe_ev.at(j, 0))
                for c in range(KC):
                    for a in range(T):
                        ins = pe.transpose(psW[:, (c * T + a) * P:(c * T + a + 1) * P], xt[:, k, a, c * P:(c + 1) * P], ident[:])
                ins.then_inc(xe_rdy.handle, 1)

            def hidden(i, k):
                j = i * RING + k
                pe.wait_ge(xe_ev.handle, xe_ev.at(j, 1))
                pe.wait_ge(hi_copied.handle, hi_copied.at(j, 1))
                pe.wait_ge(lo_copied.handle, lo_copied.at(j, 1))
                s = k % 2
                for q in range(2):
                    pe.wait_ge(h_act.handle, h_act.at(j, q - 3))
                    for m in range(2 * q, 2 * q + 2):
                        for c in range(KC):
                            for n, (w, xs) in enumerate(((w1s_hi, xe_hi), (w1s_lo, xe_hi), (w1s_hi, xe_lo))):
                                ins = pe.matmul(bank[2 * s + q][:, (m % 2) * TR:(m % 2 + 1) * TR], w[:, s, c, m * P:(m + 1) * P],
                                                xs[:, s, c], start=(c == 0 and n == 0), stop=(c == KC - 1 and n == 2))
                    ins.then_inc(h_rdy.handle, 1)

            def expert_of(i, k):
                return pe.value_load(tile_exp[0:1, bass.ds(i * RING + k, 1)], min_val=0, max_val=E - 1)

            def expert_out(i, k, e):
                j = i * RING + k
                pe.wait_ge(h_split.handle, h_split.at(j, 2))
                pe.wait_ge(y_ev.handle, y_ev.at(j, -1))
                for a in range(T):
                    for m in range(HK):
                        for n, (hs, w) in enumerate(((h_hi, w2_hi), (h_hi, w2_lo), (h_lo, w2_hi))):
                            ins = pe.matmul(psP[:, k % 2, a * D:(a + 1) * D], hs[:, k % 2, m, a * P:(a + 1) * P],
                                            w[:, bass.ds(e, 1), m].rearrange("p e n -> p (e n)"),
                                            start=(m == 0 and n == 0), stop=(m == HK - 1 and n == 2))
                ins.then_inc(y_rdy.handle, 1)

            pe.wait_ge(table_rdy.handle, 1)
            pe.wait_ge(hi_rdy.handle, 2 * E)
            pe.wait_ge(lo_rdy.handle, len(DVE_PIECES))
            pe.wait_ge(lo_rdy_pool.handle, len(POOL_PIECES))
            tile_transposed(0, 0)
            hidden(0, 0)
            tile_transposed(0, 1)
            with pe.Fori(0, TILES // RING) as i:
                for k in range(RING):
                    hidden(i + (k + 1) // RING, (k + 1) % RING)
                    e = expert_of(i, k)
                    tile_transposed(i + (k + 2) // RING, (k + 2) % RING)
                    expert_out(i, k, e)
            for k in range(TILES % RING):
                if k + 1 < TILES % RING:
                    hidden(TILES // RING, k + 1)
                e = expert_of(TILES // RING, k)
                if k + 2 < TILES % RING:
                    tile_transposed(TILES // RING, k + 2)
                expert_out(TILES // RING, k, e)


_INS = ['x', 'ctx_1024', 'mask_Bx1x1xS2_ff0', 'g_xattn', 'g_ffn', 'L0_xattn_Wq', 'L0_xattn_bq', 'L0_xattn_Wkv', 'L0_xattn_bkv',
        'L0_xattn_Wp', 'L0_xattn_bp', 'L0_ffn_Wg', 'L0_ffn_bg', 'L0_ffn_W1', 'L0_ffn_b1', 'L0_ffn_W2', 'L0_ffn_b2']


def kernel(**inputs):
    import numpy as _np
    import concourse.bacc as _bacc
    from concourse import mybir as _mybir
    from concourse.bass_utils import run_bass_kernel_spmd as _run

    nc = _bacc.Bacc("TRN2", target_bir_lowering=False, num_devices=1)
    arrays, args = {}, []
    for name in _INS:
        a = _np.ascontiguousarray(inputs[name])
        arrays[f"in_{name}"] = a
        args.append(nc.dram_tensor(f"in_{name}", a.shape, _mybir.dt.from_np(a.dtype), kind="ExternalInput").ap())
    nb, s, d = inputs['x'].shape
    args.append(nc.dram_tensor("out_0", (nb * s + T * P, d), _mybir.dt.float32, kind="ExternalOutput").ap())
    gated_xattn_moe(nc, *args)
    r = _run(nc, [arrays], core_ids=[0])
    return r.results[0]["out_0"][0:nb * s].reshape(nb, s, d)
```
